# Optimizing a Trainium2 kernel written in Bass

```python
import numpy as np
import jax
import jax.numpy as jnp

def _softmax(x, axis=-1):
    return jax.nn.softmax(x, axis=axis)

def _gelu(x):
    return jax.nn.gelu(x, approximate=True)

def _silu(x):
    return jax.nn.silu(x)

def _sigmoid(x):
    return jax.nn.sigmoid(x)

def _layernorm(x, axis=-1, eps=1e-05):
    m = jnp.mean(x, axis=axis, keepdims=True)
    v = jnp.var(x, axis=axis, keepdims=True)
    return (x - m) / jnp.sqrt(v + eps)

def _scatter_add(tgt, idx, src, axis=0):
    return tgt.at[idx].add(src)

def _segment_sum(src, seg, n):
    return jax.ops.segment_sum(src, seg, n)
kernel_name = 'mk_sandwich_d1_jaxref_r4_d31c33'

def setup_inputs(seed: int=0):
    np.random.seed(seed)
    _w = jnp.asarray

    def _L0_attn_setup():
        import jax, jax.numpy as jnp
        import numpy as np
        B, T, D = (1, 512, 1024)
        H, G = (32, 8)
        HD = D // H
        REP = H // G
        KV_DIM = 2 * HD * G
        key = jax.random.key(seed)
        k0, k1, k2, k3 = jax.random.split(key, 4)
        x = jax.random.normal(k0, (B, T, D), dtype=jnp.float32)
        Wq = jax.random.normal(k1, (D, D), dtype=jnp.float32) * 0.02
        Wkv = jax.random.normal(k2, (D, KV_DIM), dtype=jnp.float32) * 0.02
        Wo = jax.random.normal(k3, (D, D), dtype=jnp.float32) * 0.02
        bo = jnp.zeros((D,), dtype=jnp.float32)
        return {'x': x, 'Wq': Wq, 'Wkv': Wkv, 'Wo': Wo, 'bo': bo}
    _L0_attn_in = _L0_attn_setup()

    def _L0_ffn_setup():
        import jax, jax.numpy as jnp
        import numpy as np
        GROUP = 64

        def dequantize(W_q, scale, zero):
            out, half = W_q.shape
            hi = W_q >> 4 & 15
            lo = W_q & 15
            w = jnp.stack([hi, lo], axis=-1).reshape(out, half * 2).astype(scale.dtype)
            w = w.reshape(out, -1, GROUP)
            w = (w - zero[:, :, None]) * scale[:, :, None]
            return w.reshape(out, half * 2)
        key = jax.random.key(seed)
        ks = jax.random.split(key, 10)
        hidden, inter = (1024, 2752)
        B, S = (4, 256)
        x = jax.random.normal(ks[0], (B, S, hidden), dtype=jnp.float32)
        gate_Wq = jax.random.randint(ks[1], (inter, hidden // 2), 0, 64, dtype=jnp.int32)
        up_Wq = jax.random.randint(ks[2], (inter, hidden // 2), 0, 64, dtype=jnp.int32)
        down_Wq = jax.random.randint(ks[3], (hidden, inter // 2), 0, 64, dtype=jnp.int32)
        gate_scale = jax.random.uniform(ks[4], (inter, hidden // GROUP)) * 0.01 + 0.0001
        gate_zero = jax.random.uniform(ks[5], (inter, hidden // GROUP)) * 15.0
        up_scale = jax.random.uniform(ks[6], (inter, hidden // GROUP)) * 0.01 + 0.0001
        up_zero = jax.random.uniform(ks[7], (inter, hidden // GROUP)) * 15.0
        down_scale = jax.random.uniform(ks[8], (hidden, inter // GROUP)) * 0.01 + 0.0001
        down_zero = jax.random.uniform(ks[9], (hidden, inter // GROUP)) * 15.0
        return {'x': x, 'gate_Wq': gate_Wq, 'up_Wq': up_Wq, 'down_Wq': down_Wq, 'gate_scale': gate_scale, 'gate_zero': gate_zero, 'up_scale': up_scale, 'up_zero': up_zero, 'down_scale': down_scale, 'down_zero': down_zero}
    _L0_ffn_in = _L0_ffn_setup()
    _d = {'L0_attn_x': _L0_attn_in['x'], 'L0_attn_Wq': _L0_attn_in['Wq'], 'L0_attn_Wkv': _L0_attn_in['Wkv'], 'L0_attn_Wo': _L0_attn_in['Wo'], 'L0_attn_bo': _L0_attn_in['bo'], 'L0_ffn_gate_Wq': _L0_ffn_in['gate_Wq'], 'L0_ffn_up_Wq': _L0_ffn_in['up_Wq'], 'L0_ffn_down_Wq': _L0_ffn_in['down_Wq'], 'L0_ffn_gate_scale': _L0_ffn_in['gate_scale'], 'L0_ffn_gate_zero': _L0_ffn_in['gate_zero'], 'L0_ffn_up_scale': _L0_ffn_in['up_scale'], 'L0_ffn_up_zero': _L0_ffn_in['up_zero'], 'L0_ffn_down_scale': _L0_ffn_in['down_scale'], 'L0_ffn_down_zero': _L0_ffn_in['down_zero']}
    _x0 = _d['L0_attn_x']
    _d['L0_attn_x'] = jax.random.normal(jax.random.fold_in(jax.random.key(seed), 1), (1, 2048, 1024), dtype=_x0.dtype)
    del _x0
    return _d

def reference(L0_attn_x, L0_attn_Wq, L0_attn_Wkv, L0_attn_Wo, L0_attn_bo, L0_ffn_gate_Wq, L0_ffn_up_Wq, L0_ffn_down_Wq, L0_ffn_gate_scale, L0_ffn_gate_zero, L0_ffn_up_scale, L0_ffn_up_zero, L0_ffn_down_scale, L0_ffn_down_zero):

    def _L0_attn_ref(x, Wq, Wkv, Wo, bo):
        import jax, jax.numpy as jnp
        import numpy as np
        B, T, D = (1, 512, 1024)
        H, G = (32, 8)
        HD = D // H
        REP = H // G
        KV_DIM = 2 * HD * G
        b, t, d = x.shape
        q = jnp.dot(x, Wq).reshape(b, t, H, HD).transpose(0, 2, 1, 3)
        kv = jnp.dot(x, Wkv).reshape(b, t, G, 2, HD).transpose(2, 3, 0, 1, 4)
        k, v = (kv[:, 0], kv[:, 1])
        k = jnp.broadcast_to(k[:, :, None], (G, b, REP, t, HD)).reshape(b, H, t, HD)
        v = jnp.broadcast_to(v[:, :, None], (G, b, REP, t, HD)).reshape(b, H, t, HD)
        scores = jnp.einsum('bhqd,bhkd->bhqk', q, k)
        causal = jnp.triu(jnp.ones((t, t), dtype=bool), 1)
        scores = jnp.where(causal[None, None], -jnp.inf, scores)
        weights = jax.nn.softmax(scores * (1.0 / HD ** 0.5), axis=-1)
        ctx = jnp.einsum('bhqk,bhkd->bhqd', weights, v)
        ctx = ctx.transpose(0, 2, 1, 3).reshape(b, t, d)
        return jnp.dot(ctx, Wo) + bo

    def _L0_ffn_ref(x, gate_Wq, up_Wq, down_Wq, gate_scale, gate_zero, up_scale, up_zero, down_scale, down_zero):
        import jax, jax.numpy as jnp
        import numpy as np
        GROUP = 64

        def dequantize(W_q, scale, zero):
            out, half = W_q.shape
            hi = W_q >> 4 & 15
            lo = W_q & 15
            w = jnp.stack([hi, lo], axis=-1).reshape(out, half * 2).astype(scale.dtype)
            w = w.reshape(out, -1, GROUP)
            w = (w - zero[:, :, None]) * scale[:, :, None]
            return w.reshape(out, half * 2)
        Wg = dequantize(gate_Wq, gate_scale, gate_zero)
        Wu = dequantize(up_Wq, up_scale, up_zero)
        Wd = dequantize(down_Wq, down_scale, down_zero)
        g = jnp.einsum('bsh,ih->bsi', x, Wg)
        u = jnp.einsum('bsh,ih->bsi', x, Wu)
        h = jax.nn.silu(g) * u
        return jnp.einsum('bsi,hi->bsh', h, Wd)
    x = L0_attn_x
    x = x + _layernorm(_L0_attn_ref(_layernorm(x, axis=-1), L0_attn_Wq, L0_attn_Wkv, L0_attn_Wo, L0_attn_bo), axis=-1)
    x = x + _layernorm(_L0_ffn_ref(_layernorm(x, axis=-1), L0_ffn_gate_Wq, L0_ffn_up_Wq, L0_ffn_down_Wq, L0_ffn_gate_scale, L0_ffn_gate_zero, L0_ffn_up_scale, L0_ffn_up_zero, L0_ffn_down_scale, L0_ffn_down_zero), axis=-1)
    return x

_drawn_inputs = setup_inputs


def setup_inputs(seed=0):
    import zlib

    import numpy as np

    out = dict(_drawn_inputs(seed))
    spreads = {'L0_attn_bo': (0.0, 0.1)}
    factors = {}
    for name, (base, spread) in spreads.items():
        noise = np.random.default_rng([zlib.crc32(name.encode()), seed]).standard_normal(out[name].shape)
        drawn = base * np.exp(spread * noise) if base else spread * noise
        out[name] = jnp.asarray(drawn.astype(out[name].dtype))
    for name, factor in factors.items():
        out[name] = (out[name] * factor).astype(out[name].dtype)
    return out
```

```python
from contextlib import ExitStack

import concourse.bass as bass
from concourse import mybir

P = 128
BANK = 512
F32, F16, BF16, I32 = mybir.dt.float32, mybir.dt.float16, mybir.dt.bfloat16, mybir.dt.int32
ALU = mybir.AluOpType
ACT = mybir.ActivationFunctionType
AX = mybir.AxisListType

EPS = 1e-5
HEADS, GROUPS = 32, 8
QGROUP = 64
XS = 16.0
WS = 1024.0
QS = 16.0
CS = 64.0
HS = 16.0
MS = QS * QS
MASKED = -1.0e30
LEAST = -3.0e38


def build_constants(nc, ident, identb, causal, ones, sem):
    zeroed, made = sem("consts_zeroed"), sem("consts_made")
    with nc.Block() as block:
        @block.gpsimd
        def _(pool):
            nc.gpsimd.memset(ident[:], 0.0)
            nc.gpsimd.memset(identb[:], 0.0)
            nc.gpsimd.memset(ones[:], 1.0)
            nc.gpsimd.memset(causal[:], 0.0).then_inc(zeroed, 1)
            pool.wait_ge(zeroed, 1)
            for m in (ident, identb):
                nc.gpsimd.affine_select(out=m[:], in_=m[:], compare_op=ALU.not_equal, fill=1.0, base=0,
                                        pattern=[[-1, P]], channel_multiplier=1)
            nc.gpsimd.affine_select(out=causal[:], in_=causal[:], compare_op=ALU.is_ge, fill=MASKED, base=0,
                                    pattern=[[-1, P]], channel_multiplier=1).then_inc(made, 1)


class RowNorm:

    def __init__(self, nc, ctx, sem, name, in_scale, out_scale):
        self.nc = nc
        self.keep, self.root_scale = in_scale ** -2, (in_scale / out_scale) ** 2
        sb = lambda n, s: ctx.enter_context(nc.sbuf_tensor(f"{name}_{n}", s, F32))
        self.stats, self.mv = sb("stats", [P, 2, 2, 6]), sb("mv", [P, 2, 2])
        self.var, self.root, self.rstd = sb("var", [P, 2]), sb("root", [P, 2]), sb("rstd", [P, 2])
        self.stats_done, self.stats_seen, self.aggr_done, self.var_done, self.root_done, self.rstd_done = (
            sem(f"{name}_{n}") for n in
            ("stats_done", "stats_seen", "aggr_done", "var_done", "root_done", "rstd_done"))

    def on_vector(self, dve, r, wait_source, source, target, done):
        nc = self.nc
        for s in range(2):
            wait_source(s)
            rows = source(s)
            half = rows.shape[-1] // 2
            nc.vector.bn_stats(self.stats[:, s, 0, :], rows[:, 0:half])
            nc.vector.bn_stats(self.stats[:, s, 1, :], rows[:, half:]).then_inc(self.stats_done, 1)
        dve.wait_ge(self.stats_done, 2 * r + 2)
        dve.sem_inc(self.stats_seen, 1)
        for s in range(2):
            nc.vector.bn_aggr(self.mv[:, s, :], self.stats[:, s, :, :]).then_inc(self.aggr_done, 1)
        dve.wait_ge(self.aggr_done, 2 * r + 2)
        nc.vector.tensor_scalar(self.var[:], self.mv[:, :, 1], self.keep, EPS, ALU.mult, ALU.add
                                ).then_inc(self.var_done, 1)
        dve.wait_ge(self.root_done, r + 1)
        nc.vector.reciprocal(self.rstd[:], self.root[:]).then_inc(self.rstd_done, 1)
        dve.wait_ge(self.rstd_done, r + 1)
        for s in range(2):
            nc.vector.tensor_scalar(target(s), source(s), self.mv[:, s, 0:1], self.rstd[:, s:s + 1],
                                    ALU.subtract, ALU.mult).then_inc(done, 1)

    def on_scalar(self, act, r):
        act.wait_ge(self.var_done, r + 1)
        self.nc.scalar.activation(self.root[:], self.var[:], ACT.Sqrt, scale=self.root_scale
                                  ).then_inc(self.root_done, 1)


def normalise_and_load_weights(nc, x, wq, wkv, ident, x_hi, x_lo, w_hi, w_lo, sem):
    T, D = x.shape
    KC = D // P
    PAIRS = T // P // 2
    VC = wkv.shape[1] // 2
    assert PAIRS == KC
    x_loaded = [sem(f"a_x_loaded{s}") for s in range(2)]
    w_loaded, w_cut_hi, w_cut_lo = sem("a_w_loaded"), sem("a_w_cut_hi"), sem("a_w_cut_lo")
    norm_done = sem("a_norm_done")
    turned, hi_done, lo_done = sem("a_turned"), sem("a_hi_done"), sem("a_lo_done")
    with ExitStack() as ctx:
        sb = lambda n, s, d=F32: ctx.enter_context(nc.sbuf_tensor("a_" + n, s, d))
        X, XN = sb("x", [P, 2, D]), sb("xn", [P, 2, D])
        W = sb("w", [P, D + 2 * VC])
        norm = RowNorm(nc, ctx, sem, "a_norm", 1.0, XS)
        XT = ctx.enter_context(nc.psum_tensor("a_xt", [P, 2, KC * P], F32))
        block = ctx.enter_context(nc.Block())

        def of_kind(ap, kind):
            return ap.rearrange("p (g two d) -> p two g d", two=2, g=GROUPS)[:, kind]

        def columns(w, i, kind):
            at = D + kind * VC
            return w[:, i, at:at + VC].rearrange("p (g d) -> p g d", g=GROUPS)

        @block.sync
        def _(sp):
            def load_pair(i):
                for s in range(2):
                    sp.dma_start(X[:, s, :], x[bass.ds((2 * i + s) * P, P), :]).then_inc(x_loaded[s], 16)

            def load_weights(i):
                sp.dma_start(W[:, 0:D], wq[bass.ds(i * P, P), :]).then_inc(w_loaded, 16)
                sp.dma_start(W[:, D:], wkv[bass.ds(i * P, P), :]).then_inc(w_loaded, 16)
            load_pair(0)
            load_weights(0)
            with sp.Fori(0, PAIRS - 1) as i:
                sp.wait_ge(norm_done, 2 * i + 2)
                load_pair(i + 1)
                sp.wait_ge(w_cut_lo, 3 * i + 3)
                load_weights(i + 1)

        @block.vector
        def _(dve):
            with dve.Fori(0, PAIRS) as i:
                norm.on_vector(dve, i, lambda s: dve.wait_ge(x_loaded[s], 16 * i + 16),
                               lambda s: X[:, s, :], lambda s: XN[:, s, :], norm_done)
                dve.wait_ge(w_cut_hi, 3 * i + 3)
                nc.vector.scalar_tensor_tensor(w_lo[:, i, 0:D], W[:, 0:D], WS, w_hi[:, i, 0:D],
                                               ALU.mult, ALU.subtract).then_inc(w_cut_lo, 1)
                for kind in range(2):
                    nc.vector.scalar_tensor_tensor(
                        columns(w_lo, i, kind), of_kind(W[:, D:], kind), WS, columns(w_hi, i, kind),
                        ALU.mult, ALU.subtract).then_inc(w_cut_lo, 1)
                for s in range(2):
                    dve.wait_ge(hi_done, 2 * i + s + 1)
                    nc.vector.tensor_tensor(
                        x_lo[:, :, bass.ds((2 * i + s) * P, P)], XT[:, s, :].rearrange("p (c t) -> p c t", t=P),
                        x_hi[:, :, bass.ds((2 * i + s) * P, P)], ALU.subtract).then_inc(lo_done, 1)

        @block.scalar
        def _(act):
            with act.Fori(0, PAIRS) as i:
                norm.on_scalar(act, i)
                act.wait_ge(w_loaded, 32 * i + 32)
                nc.scalar.activation(w_hi[:, i, 0:D], W[:, 0:D], ACT.Copy, scale=WS).then_inc(w_cut_hi, 1)
                for kind in range(2):
                    nc.scalar.activation(columns(w_hi, i, kind), of_kind(W[:, D:], kind),
                                         ACT.Copy, scale=WS).then_inc(w_cut_hi, 1)
                for s in range(2):
                    act.wait_ge(turned, 2 * i + s + 1)
                    nc.scalar.activation(
                        x_hi[:, :, bass.ds((2 * i + s) * P, P)],
                        XT[:, s, :].rearrange("p (c t) -> p c t", t=P), ACT.Copy).then_inc(hi_done, 1)

        @block.tensor
        def _(pe):
            with pe.Fori(0, PAIRS) as i:
                for s in range(2):
                    pe.wait_ge(norm_done, 2 * i + s + 1)
                    for c in range(KC):
                        last = nc.tensor.transpose(XT[:, s, c * P:(c + 1) * P], XN[:, s, c * P:(c + 1) * P],
                                                   ident[:])
                    last.then_inc(turned, 1)


def project_qkv(nc, x_hi, x_lo, w_hi, w_lo, qk_hi, qk_lo, v_sb, sem):
    KC, T = x_hi.shape[1], x_hi.shape[2]
    QK = qk_hi.shape[0]
    NB = T // BANK
    COLS = QK // P
    VC = v_sb.shape[2]
    product, hi_done, lo_done = sem("b_product"), sem("b_hi_done"), sem("b_lo_done")
    v_product, v_done = sem("b_v_product"), sem("b_v_done")
    hi_stored = [sem(f"b_hi_stored{b}") for b in range(NB)]
    lo_stored = [sem(f"b_lo_stored{b}") for b in range(NB)]
    out_scale = QS / (XS * WS)
    with ExitStack() as ctx:
        HI = ctx.enter_context(nc.sbuf_tensor("b_hi", [P, NB, BANK], F16))
        LO = ctx.enter_context(nc.sbuf_tensor("b_lo", [P, NB, BANK], F16))
        PS = ctx.enter_context(nc.psum_tensor("b_ps", [P, NB, BANK], F32))
        VPS = ctx.enter_context(nc.psum_tensor("b_vps", [P, 4, BANK], F32))
        block = ctx.enter_context(nc.Block())

        @block.tensor
        def _(pe):
            def column_tile(c, first):
                for b in range(NB):
                    if not first:
                        pe.wait_ge(lo_done, NB * c + b + 1 - NB)
                    for k in range(KC):
                        wh, wl = w_hi[:, k, bass.ds(c * P, P)], w_lo[:, k, bass.ds(c * P, P)]
                        xh, xl = (x[:, k, b * BANK:(b + 1) * BANK] for x in (x_hi, x_lo))
                        nc.tensor.matmul(PS[:, b, :], wh, xh, start=(k == 0), stop=False)
                        nc.tensor.matmul(PS[:, b, :], wh, xl, start=False, stop=False)
                        last = nc.tensor.matmul(PS[:, b, :], wl, xh, start=False, stop=(k == KC - 1))
                    last.then_inc(product, 1)

            def value_tiles(i, first):
                for u in range(4):
                    if not first:
                        pe.wait_ge(v_done, 4 * i + u - 3)
                    for k in range(KC):
                        xh, xl = (x[:, k, bass.ds((4 * i + u) * P, P)] for x in (x_hi, x_lo))
                        wh, wl = w_hi[:, k, QK:QK + VC], w_lo[:, k, QK:QK + VC]
                        o = VPS[:, u, 0:VC]
                        nc.tensor.matmul(o, xh, wh, start=(k == 0), stop=False)
                        nc.tensor.matmul(o, xh, wl, start=False, stop=False)
                        last = nc.tensor.matmul(o, xl, wh, start=False, stop=(k == KC - 1))
                    last.then_inc(v_product, 1)
            column_tile(0, True)
            with pe.Fori(1, COLS) as c:
                column_tile(c, False)
            value_tiles(0, True)
            with pe.Fori(1, T // P // 4) as i:
                value_tiles(i, False)

        @block.scalar
        def _(act):
            def column_tile(c, first):
                for b in range(NB):
                    if not first:
                        act.wait_ge(hi_stored[b], 16 * c)
                    act.wait_ge(product, NB * c + b + 1)
                    nc.scalar.activation(HI[:, b, :], PS[:, b, :], ACT.Copy, scale=out_scale).then_inc(hi_done, 1)
            column_tile(0, True)
            with act.Fori(1, COLS) as c:
                column_tile(c, False)

        @block.vector
        def _(dve):
            def column_tile(c, first):
                for b in range(NB):
                    if not first:
                        dve.wait_ge(lo_stored[b], 16 * c)
                    dve.wait_ge(hi_done, NB * c + b + 1)
                    nc.vector.scalar_tensor_tensor(LO[:, b, :], PS[:, b, :], out_scale, HI[:, b, :],
                                                   ALU.mult, ALU.subtract).then_inc(lo_done, 1)
            column_tile(0, True)
            with dve.Fori(1, COLS) as c:
                column_tile(c, False)
            with dve.Fori(0, T // P // 4) as i:
                for u in range(4):
                    dve.wait_ge(v_product, 4 * i + u + 1)
                    nc.vector.tensor_scalar(v_sb[:, 4 * i + u, :], VPS[:, u, 0:VC], 1.0 / (XS * WS), None,
                                            ALU.mult).then_inc(v_done, 1)

        @block.sync
        def _(sp):
            with sp.Fori(0, COLS) as c:
                for b in range(NB):
                    sp.wait_ge(hi_done, NB * c + b + 1)
                    sp.dma_start(qk_hi[bass.ds(c * P, P), b * BANK:(b + 1) * BANK], HI[:, b, :]
                                 ).then_inc(hi_stored[b], 16)
                    sp.wait_ge(lo_done, NB * c + b + 1)
                    sp.dma_start(qk_lo[bass.ds(c * P, P), b * BANK:(b + 1) * BANK], LO[:, b, :]
                                 ).then_inc(lo_stored[b], 16)
            for b in range(NB):
                sp.wait_ge(hi_stored[b], 16 * COLS)
                sp.wait_ge(lo_stored[b], 16 * COLS)


def attend(nc, qk_hi, qk_lo, v_sb, ident, identb, causal, ones, c_hi, c_lo, sem):
    T = qk_hi.shape[1]
    D = c_hi.shape[1] * P
    HD = D // HEADS
    NT, NB, REP = T // P, T // BANK, HEADS // GROUPS
    TPB = BANK // P
    STACK = 3 * HD
    UNIT = 2 * BANK
    RING = 5
    exp_scale = float(HD) ** -0.5 / MS

    steps = [(b, k) for b in range(NB) for k in range(TPB * (b + 1))]
    STEPS = len(steps)
    last_of = {s: b for s, (b, k) in enumerate(steps) if k == TPB * (b + 1) - 1}
    assert T == 2 * UNIT
    half = NT // 2
    units = [unit for h in range(REP) for a in range(half)
             for unit in ((h, half + a, 0), (h, a, 0), (h, NT - 1 - a, 1))]
    UNITS = len(units)
    SLOTS = UNITS + 1
    width = [BANK - max(0, k - TPB * b) * P for b, k in steps]
    TURN = STEPS - 3
    share = [min(UNITS, -(-UNITS * sum(width[:s]) // sum(width[:TURN]))) for s in range(STEPS + 1)]
    units_in = [range(share[s], share[s + 1]) for s in range(STEPS)]

    sums_of_block, place_of, pairs = [], {}, []
    for b in range(NB):
        first = TPB * b * (b + 1) // 2
        last, at = first + TPB * (b + 1) - 1, 0
        for a in range(first, last, 2):
            if a + 1 == last or (b == NB - 1 and a == last - 3):
                alone = [(a, 1), (a + 1, 1)]
            else:
                alone = [(a, 2)]
                pairs.append(a)
            for first_step, count in alone:
                at = max(at, first_step + (1 if count == 1 else 4))
                place_of[first_step] = at
                sums_of_block.append((b, first_step, count))
    sum_order = sorted(sums_of_block, key=lambda e: (place_of[e[1]], e[1]))
    SUMS = len(sum_order)
    sum_of_step = {a + i: n for n, (_, a, count) in enumerate(sum_order) for i in range(count)}
    last_sum = {b: max(n for n, e in enumerate(sum_order) if e[0] == b) for b in range(NB)}
    first_sum = {b: min(n for n, e in enumerate(sum_order) if e[0] == b) for b in range(NB)}

    def sums_in(s):
        return [n for n, e in enumerate(sum_order) if place_of[e[1]] == s]

    added = sem("c_added")
    sums_done = sem("c_sums_done")
    loaded, max_stored, buffer_free = sem("c_loaded"), sem("c_max_stored"), sem("c_buffer_free")
    unit_done, maxed, max_done = sem("c_unit_done"), sem("c_maxed"), sem("c_max_done")
    scores_done, exp_done, pv_done = sem("c_scores_done"), sem("c_exp_done"), sem("c_pv_done")
    ctx_read, sum_read, normed = sem("c_ctx_read"), sem("c_sum_read"), sem("c_normed")
    inverted, values_ready = sem("c_inverted"), sem("c_values_ready")
    ctx_hi_done, ctx_lo_done, filled = sem("c_ctx_hi_done"), sem("c_ctx_lo_done"), sem("c_filled")
    S2_FREE, PROB_FREE, SUM_FREE, C_FREE, CN_FREE = 2, SUMS, 1, 2, 2

    with ExitStack() as ctx:
        sb = lambda n, s, d=F32: ctx.enter_context(nc.sbuf_tensor("c_" + n, s, d))
        ps = lambda n, s, d=F32: ctx.enter_context(nc.psum_tensor("c_" + n, s, d))
        Q, K = sb("q", [STACK + 1, 3, REP, T], F16), sb("k", [STACK + 1, 3, T], F16)
        V = sb("v", [P, NT, HD])
        PROB = sb("prob", [P, RING * REP, BANK])
        MAXES, NEGMAX = sb("maxes", [P, NT * REP, 2]), sb("negmax", [P, P])
        MROW = sb("mrow", [NT * REP, P], F16)
        C, R, CN = sb("c", [P, 2, BANK]), sb("r", [P, BANK]), sb("cn", [P, 2, BANK])
        S1 = ps("s1", [P, 2, UNIT])
        S2 = ps("s2", [P, 2, BANK])
        CTX, SUM = ps("ctx", [P, BANK]), ps("sum", [P, BANK])
        block = ctx.enter_context(nc.Block())

        def diagonal(s):
            b, k = steps[s]
            return max(0, k - TPB * b) * P, k >= TPB * b

        @block.sync
        def _(sp):
            def load_group(g, buf):
                qrows, krows = bass.ds(g * P, P), bass.ds(D + g * HD, HD)
                for row, (qs, ks) in enumerate(((qk_hi, qk_hi), (qk_lo, qk_hi), (qk_hi, qk_lo))):
                    part = slice(row * HD, (row + 1) * HD)
                    sp.dma_start(Q[part, buf], qs[qrows, :].rearrange("(h d) t -> d h t", d=HD)
                                 ).then_inc(loaded, 16)
                    sp.dma_start(K[part, buf], ks[krows, :]).then_inc(loaded, 16)

            def store_maxima(g, buf):
                sp.wait_ge(maxed, SLOTS * g + SLOTS)
                sp.dma_start(Q[STACK:STACK + 1, buf].rearrange("o h (t q) -> o (h t) q", q=P),
                             MROW[:, :]).then_inc(max_stored, 16)
            load_group(0, 0)
            sp.wait_ge(loaded, 96)
            load_group(1, 1)
            store_maxima(0, 0)
            sp.wait_ge(loaded, 192)
            load_group(2, 2)
            store_maxima(1, 1)
            with sp.Fori(1, GROUPS - 2) as g:
                sp.wait_ge(loaded, 96 * g + 192)
                sp.sem_inc(buffer_free, 1)
                sp.wait_ge(scores_done, REP * STEPS * g)
                sp.sem_inc(buffer_free, 1)
                load_group(g + 2, (g + 2) % 3)
                store_maxima(g + 1, (g + 1) % 3)
            store_maxima(GROUPS - 1, (GROUPS - 1) % 3)

        def bodies(eng, body, ahead):
            ahead()
            with eng.Fori(0, GROUPS - 1) as g:
                body(g, True)
            body(GROUPS - 1, False)

        @block.tensor
        def _(pe):
            def unit(g, n):
                h, t, u = units[n]
                buf, slot = g % 3, n % 2
                free = SLOTS * g + (n - 1 if n else 0)
                if not (isinstance(free, int) and free <= 0):
                    pe.wait_ge(maxed, free)
                end = min(UNIT, (t + 1) * P - u * UNIT)
                for c in range(0, end, BANK):
                    n_c = min(BANK, end - c)
                    diag = u * UNIT + c + n_c == (t + 1) * P
                    last = nc.tensor.matmul(S1[:, slot, c:c + n_c], Q[0:STACK, buf, h, t * P:(t + 1) * P],
                                            K[0:STACK, buf, u * UNIT + c:u * UNIT + c + n_c],
                                            start=True, stop=not diag)
                    if diag:
                        last = nc.tensor.matmul(S1[:, slot, c + n_c - P:c + n_c], identb[:], causal[:],
                                                start=False, stop=True)
                last.then_inc(unit_done, 1)

            def turn_maxima(g):
                pe.wait_ge(max_done, g + 1)
                nc.tensor.transpose(S1[:, 0, 0:P], NEGMAX[:, :], ident[:]).then_inc(unit_done, 1)

            def scores(g, s, heads):
                b, k = steps[s]
                j, diag = diagonal(s)
                buf = g % 3
                for h in heads:
                    n = REP * STEPS * g + REP * s + h
                    pe.wait_ge(exp_done, n - 1 + S2_FREE)
                    last = nc.tensor.matmul(S2[:, h % 2, j:BANK], K[:, buf, k * P:(k + 1) * P],
                                            Q[:, buf, h, b * BANK + j:(b + 1) * BANK], start=True, stop=not diag)
                    if diag:
                        last = nc.tensor.matmul(S2[:, h % 2, j:j + P], causal[:], identb[:], start=False, stop=True)
                    last.then_inc(scores_done, 1)

            def products(g, s):
                b, k = steps[s]
                j, _ = diagonal(s)
                if s == 0:
                    pe.wait_ge(values_ready, g + 1)
                pe.wait_ge(exp_done, REP * STEPS * g + REP * s + REP + S2_FREE)
                if k == 0:
                    pe.wait_ge(ctx_read, NB * g + b + SUM_FREE)
                for h in range(REP):
                    last = nc.tensor.matmul(CTX[h * HD:(h + 1) * HD, j:BANK], V[:, k, :],
                                            PROB[:, REP * (s % RING) + h, j:BANK],
                                            start=(k == 0), stop=(k == TPB * (b + 1) - 1))
                last.then_inc(pv_done, 1)

            def sums(g, place):
                for n in sums_in(place):
                    b, s, count = sum_order[n]
                    j, _ = diagonal(s)
                    if n == first_sum[b]:
                        pe.wait_ge(sum_read, NB * g + b + SUM_FREE)
                    if count == 2:
                        pe.wait_ge(added, len(pairs) * g + pairs.index(s) + 1)
                    for h in range(REP):
                        last = nc.tensor.matmul(SUM[h * HD:(h + 1) * HD, j:BANK], ones[:],
                                                PROB[:, REP * (s % RING) + h, j:BANK],
                                                start=(n == first_sum[b]), stop=(n == last_sum[b]))
                    last.then_inc(sums_done, 1)

            def ahead():
                pe.sem_inc(sums_done, PROB_FREE)
                pe.wait_ge(loaded, 96)
                for n in range(UNITS):
                    unit(0, n)
                turn_maxima(0)

            def body(g, first_pass):
                pe.wait_ge(max_stored, 16 * g + 16)
                if first_pass:
                    pe.wait_ge(loaded, 96 * g + 192)

                def some_units(s, third):
                    if first_pass:
                        n = units_in[s]
                        for i in n[len(n) * third // 3:len(n) * (third + 1) // 3]:
                            unit(g + 1, i)
                for s in range(STEPS):
                    scores(g, s, (0, 1))
                    some_units(s, 0)
                    if s:
                        products(g, s - 1)
                    some_units(s, 1)
                    scores(g, s, (2, 3))
                    sums(g, s)
                    some_units(s, 2)
                    if first_pass and s == TURN:
                        turn_maxima(g + 1)
                products(g, STEPS - 1)
                sums(g, STEPS)
            bodies(pe, body, ahead)

        @block.scalar
        def _(act):
            act.sem_inc(exp_done, S2_FREE)
            act.sem_inc(ctx_read, SUM_FREE)

            def read_context(g, b, s):
                act.wait_ge(pv_done, STEPS * g + s + 1)
                act.wait_ge(normed, NB * g + b - 1 + C_FREE)
                nc.scalar.activation(C[:, b % 2, :], CTX[:, :], ACT.Copy, scale=CS).then_inc(ctx_read, 1)
            with act.Fori(0, GROUPS) as g:
                for s in range(STEPS):
                    j, _ = diagonal(s)
                    before = sum_of_step[s - RING] + SUMS if s >= RING else sum_of_step[s - RING + STEPS]
                    act.wait_ge(sums_done, SUMS * g + before + 1)
                    for h in range(REP):
                        act.wait_ge(scores_done, REP * STEPS * g + REP * s + h + 1)
                        nc.scalar.activation(PROB[:, REP * (s % RING) + h, j:BANK], S2[:, h % 2, j:BANK], ACT.Exp,
                                             scale=exp_scale).then_inc(exp_done, 1)
                    if s - 1 in last_of:
                        read_context(g, last_of[s - 1], s - 1)
                read_context(g, NB - 1, STEPS - 1)

        @block.vector
        def _(dve):
            def unit(g, n):
                h, t, u = units[n]
                end = min(UNIT, (t + 1) * P - u * UNIT)
                dve.wait_ge(unit_done, SLOTS * g + n + 1)
                nc.vector.tensor_reduce(MAXES[:, h * NT + t, u:u + 1], S1[:, n % 2, 0:end],
                                        AX.X, ALU.max).then_inc(maxed, 1)

            def join_maxima(g):
                dve.wait_ge(maxed, SLOTS * g + UNITS)
                nc.vector.tensor_reduce(NEGMAX[:, 0:NT * REP], MAXES[:, :, :], AX.X, ALU.max, negate=True
                                        ).then_inc(max_done, 1)

            def write_maxima(g):
                if not (isinstance(g, int) and g == 0):
                    dve.wait_ge(max_stored, 16 * g)
                dve.wait_ge(unit_done, SLOTS * g + SLOTS)
                nc.vector.tensor_scalar(MROW[:, :], S1[0:NT * REP, 0, 0:P], 1.0 / MS, None, ALU.mult
                                        ).then_inc(maxed, 1)

            def ahead():
                dve.sem_inc(sum_read, SUM_FREE)
                dve.sem_inc(normed, C_FREE)
                nc.vector.memset(MAXES[:], LEAST)
                nc.vector.memset(NEGMAX[:], 0.0)
                nc.vector.memset(K[STACK:STACK + 1, :, :], MS).then_inc(filled, 1)
                dve.wait_ge(filled, 1)
                for n in range(UNITS):
                    unit(0, n)
                join_maxima(0)
                write_maxima(0)

            PIECES = 4
            piece = BANK // PIECES

            def invert_piece(g, b, i):
                n = NB * g + b
                if i == 0:
                    dve.wait_ge(sums_done, SUMS * g + last_sum[b] + 1 + PROB_FREE)
                    dve.wait_ge(normed, n + C_FREE)
                at = slice(i * piece, (i + 1) * piece)
                last = nc.vector.reciprocal(R[:, at], SUM[:, at])
                if i == PIECES - 1:
                    last.then_inc(sum_read, 1)

            def normalise(g, b):
                n = NB * g + b
                dve.wait_ge(ctx_lo_done, n - 1 + CN_FREE)
                dve.wait_ge(ctx_read, n + 1 + SUM_FREE)
                dve.wait_ge(sum_read, n + 1 + SUM_FREE)
                nc.vector.tensor_tensor(CN[:, b % 2, :], C[:, b % 2, :], R[:], ALU.mult).then_inc(normed, 1)

            def body(g, first_pass, first_group):
                left = [] if first_group else [(g - 1, NB - 1, i) for i in range(PIECES + 1)]

                def one_piece():
                    if left:
                        of, b, i = left.pop(0)
                        if i < PIECES:
                            invert_piece(of, b, i)
                        else:
                            normalise(of, b)
                if first_pass:
                    dve.wait_ge(max_done, g + 1)
                for s in range(STEPS):
                    if s - 2 in last_of:
                        left += [(g, last_of[s - 2], i) for i in range(PIECES + 1)]
                    one_piece()
                    if first_pass:
                        for n in units_in[s]:
                            unit(g + 1, n)
                            if n == UNITS - 1:
                                join_maxima(g + 1)
                        if s == TURN:
                            write_maxima(g + 1)
                assert not left
            ahead()
            body(0, True, True)
            with dve.Fori(1, GROUPS - 1) as g:
                body(g, True, False)
            body(GROUPS - 1, False, False)
            for i in range(PIECES):
                invert_piece(GROUPS - 1, NB - 1, i)
            normalise(GROUPS - 1, NB - 1)

        @block.gpsimd
        def _(pool):
            def take_values(g):
                nc.gpsimd.tensor_copy(V[:, :, :], v_sb[:, :, bass.ds(g * HD, HD)]).then_inc(values_ready, 1)

            def cut_context(g, b):
                n = NB * g + b
                at = slice(b * BANK, (b + 1) * BANK)
                pool.wait_ge(normed, n + 1 + C_FREE)
                nc.gpsimd.tensor_copy(c_hi[:, g, at], CN[:, b % 2, :]).then_inc(ctx_hi_done, 1)
                pool.wait_ge(ctx_hi_done, n + 1)
                nc.gpsimd.tensor_tensor(c_lo[:, g, at], CN[:, b % 2, :], c_hi[:, g, at], ALU.subtract
                                        ).then_inc(ctx_lo_done, 1)
            def add_pair(g, n):
                a = pairs[n]
                j, _ = diagonal(a + 1)
                pool.wait_ge(pv_done, STEPS * g + a + 1)
                pool.wait_ge(exp_done, REP * (STEPS * g + a + 2) + S2_FREE)
                for h in range(REP):
                    one, two = (PROB[:, REP * (t % RING) + h, j:BANK] for t in (a, a + 1))
                    last = nc.gpsimd.tensor_tensor(one, one, two, ALU.add)
                last.then_inc(added, 1)
            pool.sem_inc(ctx_lo_done, CN_FREE)
            take_values(0)
            def body(g, first_group):
                cuts = {}
                for b in range(NB - 1):
                    last = TPB * (b + 1) * (b + 2) // 2 - 1
                    cuts[min(a for a in pairs if a >= last + 5)] = (g, b)
                for n, a in enumerate(pairs):
                    if a in cuts:
                        cut_context(*cuts[a])
                    add_pair(g, n)
                    if n == 0 and not first_group:
                        cut_context(g - 1, NB - 1)
                pool.wait_ge(pv_done, STEPS * g + STEPS)
                take_values((g + 1) % GROUPS)
            body(0, True)
            with pool.Fori(1, GROUPS) as g:
                body(g, False)
            cut_context(GROUPS - 1, NB - 1)


def project_context(nc, c_hi, c_lo, wo, bo, x, x1_dram, ident, x2_hi, x2_lo, sem):
    KC, T = c_hi.shape[1], c_hi.shape[2]
    D = KC * P
    PAIRS = T // P // 2
    wo_loaded, bo_loaded = [sem(f"d_wo_loaded{s}") for s in range(2)], sem("d_bo_loaded")
    wo_cut_hi, wo_cut_lo = sem("d_wo_cut_hi"), sem("d_wo_cut_lo")
    x_loaded, x1_stored = [sem(f"d_x_loaded{s}") for s in range(2)], [sem(f"d_x1_stored{s}") for s in range(2)]
    y_product, y_read, y_normed, x1_done = sem("d_y_product"), sem("d_y_read"), sem("d_y_normed"), sem("d_x1_done")
    norm_done, turned, hi_done, lo_done = sem("d_norm_done"), sem("d_turned"), sem("d_hi_done"), sem("d_lo_done")
    with ExitStack() as ctx:
        sb = lambda n, s, d=F32: ctx.enter_context(nc.sbuf_tensor("d_" + n, s, d))
        WO, BO = sb("wo", [P, 2, D]), sb("bo", [P, D])
        wo_hi, wo_lo = sb("wo_hi", [P, KC, D], F16), sb("wo_lo", [P, KC, D], F16)
        X, Y, X1, XN = (sb(n, [P, 2, D]) for n in ("x", "y", "x1", "xn"))
        y_norm = RowNorm(nc, ctx, sem, "d_y_norm", 1.0, 1.0)
        x_norm = RowNorm(nc, ctx, sem, "d_x_norm", 1.0, XS)
        YP = ctx.enter_context(nc.psum_tensor("d_yp", [P, 2, D], F32))
        XT = ctx.enter_context(nc.psum_tensor("d_xt", [P, 2, D], F32))
        block = ctx.enter_context(nc.Block())

        def tokens(i, s):
            return bass.ds((2 * i + s) * P, P)

        @block.sync
        def _(sp):
            def load_weights(k):
                sp.dma_start(WO[:, k % 2, :], wo[k * P:(k + 1) * P, :]).then_inc(wo_loaded[k % 2], 16)

            def load_rows(i):
                for s in range(2):
                    sp.dma_start(X[:, s, :], x[tokens(i, s), :]).then_inc(x_loaded[s], 16)

            def store_rows(i):
                for s in range(2):
                    sp.wait_ge(x1_done, 2 * i + s + 1)
                    sp.dma_start(x1_dram[tokens(i, s), :], X1[:, s, :]).then_inc(x1_stored[s], 16)
            load_weights(0)
            load_weights(1)
            sp.dma_start(BO[:], bo.rearrange("(o n) -> o n", o=1).broadcast_to([P, D])).then_inc(bo_loaded, 16)
            load_rows(0)
            for k in range(2, KC):
                sp.wait_ge(wo_cut_lo, k - 1)
                load_weights(k)
            with sp.Fori(0, PAIRS - 1) as i:
                store_rows(i)
                load_rows(i + 1)
            store_rows(PAIRS - 1)
            for s in range(2):
                sp.wait_ge(x1_stored[s], 16 * PAIRS)

        @block.tensor
        def _(pe):
            def product(i, first=False):
                for s in range(2):
                    if not first:
                        pe.wait_ge(y_read, 2 * i + s - 1)
                    for k in range(KC):
                        if first and s == 0:
                            pe.wait_ge(wo_cut_lo, k + 1)
                        ch, cl = (c[:, k, tokens(i, s)] for c in (c_hi, c_lo))
                        for stat, w, a, z in ((ch, wo_hi, 1, 0), (ch, wo_lo, 0, 0), (cl, wo_hi, 0, 1)):
                            for n in range(0, D, BANK):
                                last = nc.tensor.matmul(YP[:, s, n:n + BANK], stat, w[:, k, n:n + BANK],
                                                        start=(k == 0 and a == 1), stop=(k == KC - 1 and z == 1))
                    last.then_inc(y_product, 1)

            def turn(i):
                for s in range(2):
                    pe.wait_ge(norm_done, 2 * i + s + 1)
                    for c in range(KC):
                        last = nc.tensor.transpose(XT[:, s, c * P:(c + 1) * P], XN[:, s, c * P:(c + 1) * P],
                                                   ident[:])
                    last.then_inc(turned, 1)
            product(0, True)
            with pe.Fori(0, PAIRS - 1) as i:
                product(i + 1)
                turn(i)
            turn(PAIRS - 1)

        @block.vector
        def _(dve):
            for k in range(KC):
                dve.wait_ge(wo_cut_hi, k + 1)
                nc.vector.scalar_tensor_tensor(wo_lo[:, k, :], WO[:, k % 2, :], WS, wo_hi[:, k, :],
                                               ALU.mult, ALU.subtract).then_inc(wo_cut_lo, 1)
            dve.wait_ge(bo_loaded, 16)
            with dve.Fori(0, PAIRS) as i:
                for s in range(2):
                    dve.wait_ge(y_product, 2 * i + s + 1)
                    nc.vector.scalar_tensor_tensor(Y[:, s, :], YP[:, s, :], 1.0 / (CS * WS), BO[:],
                                                   ALU.mult, ALU.add).then_inc(y_read, 1)
                y_norm.on_vector(dve, i, lambda s: dve.wait_ge(y_read, 2 * i + s + 1),
                                 lambda s: Y[:, s, :], lambda s: Y[:, s, :], y_normed)
                x_norm.on_vector(dve, i, lambda s: dve.wait_ge(x1_done, 2 * i + s + 1),
                                 lambda s: X1[:, s, :], lambda s: XN[:, s, :], norm_done)
                for s in range(2):
                    dve.wait_ge(hi_done, 2 * i + s + 1)
                    nc.vector.tensor_tensor(x2_lo[:, :, tokens(i, s)], XT[:, s, :].rearrange("p (c t) -> p c t", t=P),
                                            x2_hi[:, :, tokens(i, s)], ALU.subtract).then_inc(lo_done, 1)

        @block.scalar
        def _(act):
            for k in range(KC):
                act.wait_ge(wo_loaded[k % 2], 16 * (k // 2) + 16)
                nc.scalar.activation(wo_hi[:, k, :], WO[:, k % 2, :], ACT.Copy, scale=WS).then_inc(wo_cut_hi, 1)
            with act.Fori(0, PAIRS) as i:
                y_norm.on_scalar(act, i)
                x_norm.on_scalar(act, i)
                for s in range(2):
                    act.wait_ge(turned, 2 * i + s + 1)
                    nc.scalar.activation(x2_hi[:, :, tokens(i, s)], XT[:, s, :].rearrange("p (c t) -> p c t", t=P),
                                         ACT.Copy).then_inc(hi_done, 1)

        @block.gpsimd
        def _(pool):
            def residual(i, first):
                for s in range(2):
                    if not first:
                        pool.wait_ge(x1_stored[s], 16 * i)
                    pool.wait_ge(x_loaded[s], 16 * i + 16)
                    pool.wait_ge(y_normed, 2 * i + s + 1)
                    nc.gpsimd.tensor_tensor(X1[:, s, :], X[:, s, :], Y[:, s, :], ALU.add).then_inc(x1_done, 1)
            residual(0, True)
            with pool.Fori(1, PAIRS) as i:
                residual(i, False)


def gate_and_up(nc, x2_hi, x2_lo, quantised, ident, wd_hi, wd_lo, h_hi, h_lo, sem):
    KC, T = x2_hi.shape[1], x2_hi.shape[2]
    D = KC * P
    NB = T // BANK
    (gate_q, gate_s, gate_z), (up_q, up_s, up_z), (down_q, down_s, down_z) = quantised
    inter = gate_q.shape[0]
    FULL, REST = inter // P, inter % P
    CHUNKS = FULL + (REST > 0)
    assert CHUNKS % 2 == 0 and 0 < REST and REST % QGROUP == 0 and NB == 4
    GROUPS_IN, GROUPS_MID = D // QGROUP, inter // QGROUP
    GATE, UP, DOWN = range(3)
    in_scale = 1.0 / (XS * WS)

    tables_loaded, raw_loaded = sem("e_tables_loaded"), [sem(f"e_raw_loaded{s}") for s in range(2)]
    unpacked, shifted, scaled = sem("e_unpacked"), sem("e_shifted"), sem("e_scaled")
    turned, cut_hi, cut_lo = sem("e_turned"), sem("e_cut_hi"), sem("e_cut_lo")
    gate_product, up_product, silu_done = sem("e_gate_product"), sem("e_up_product"), sem("e_silu_done")
    h_done, hi_done, lo_done, cleared = (sem(f"e_{n}") for n in ("h_done", "hi_done", "lo_done", "cleared"))
    hi_stored, lo_stored = ([sem(f"e_{n}_stored{s}") for s in range(2)] for n in ("hi", "lo"))
    FREE = 2

    with ExitStack() as ctx:
        sb = lambda n, s, d=F32: ctx.enter_context(nc.sbuf_tensor("e_" + n, s, d))
        scales = [sb(f"{n}_s", [P, CHUNKS, GROUPS_IN]) for n in ("gate", "up")] + [sb("down_s", [P, KC, GROUPS_MID])]
        zeros = [sb(f"{n}_z", [P, CHUNKS, GROUPS_IN]) for n in ("gate", "up")] + [sb("down_z", [P, KC, GROUPS_MID])]
        RAW, NIBBLES = sb("raw", [P, 2, D // 2], I32), sb("nibbles", [P, D], I32)
        W = sb("w", [P, 2, D])
        w_hi, w_lo = (sb(n, [P, 2, 2, KC, P], F16) for n in ("w_hi", "w_lo"))
        SILU, H = sb("silu", [P, 2, BANK]), sb("h", [P, 2, BANK])
        HH, HL = sb("hh", [P, 2, BANK], F16), sb("hl", [P, 2, BANK], F16)
        WT = ctx.enter_context(nc.psum_tensor("e_wt", [P, 2, D], F32))
        GP = ctx.enter_context(nc.psum_tensor("e_gp", [P, 2, BANK], F32))
        UP_ = ctx.enter_context(nc.psum_tensor("e_up", [P, 2, BANK], F32))
        block = ctx.enter_context(nc.Block())

        def number(chunk):
            return 2 * chunk[0] + chunk[1]

        def height(chunk):
            c = number(chunk)
            return REST if isinstance(c, int) and c == FULL else P

        def after(chunk):
            j, parity = chunk
            return (j, 1) if parity == 0 else (j + 1, 0)

        def weights(chunk, kind):
            j, parity = chunk
            return 6 * j + 3 * parity + kind, (parity + kind) % 2

        def wait_positive(eng, signal, value):
            if not (isinstance(value, int) and value <= 0):
                eng.wait_ge(signal, value)

        def extent(kind, chunk):
            n = height(chunk)
            return (P, KC * n // 2) if kind == DOWN else (n, D // 2)

        def table(t, kind, chunk):
            n = height(chunk)
            if kind != DOWN:
                return t[kind][0:n, number(chunk), :].unsqueeze(2).broadcast_to([n, GROUPS_IN, QGROUP])
            at = bass.ds(number(chunk) * (P // QGROUP), n // QGROUP)
            return t[kind][:, :, at].unsqueeze(3).broadcast_to([P, KC, n // QGROUP, QGROUP])

        def grouped(ap, kind, chunk):
            rows, packed = extent(kind, chunk)
            flat = ap[0:rows, 0:2 * packed]
            if kind != DOWN:
                return flat.rearrange("p (g j) -> p g j", j=QGROUP)
            return flat.rearrange("p (k g j) -> p k g j", k=KC, j=QGROUP)

        def turned_parts(kind, chunk):
            n, (_, slot) = height(chunk), weights(chunk, kind)
            if kind == DOWN:
                return WT[0:n, slot, :], wd_hi[0:n, number(chunk), :], wd_lo[0:n, number(chunk), :]
            at = (slice(None), kind, chunk[1], slice(None), slice(0, n))
            return WT[:, slot, :].rearrange("p (k i) -> p k i", i=P)[:, :, 0:n], w_hi[at], w_lo[at]

        def all_chunks(eng, prepare, multiply):
            for kind in range(3):
                prepare((0, 0), kind)
            with eng.Fori(0, FULL // 2) as j:
                for parity in range(2):
                    multiply((j, parity), after((j, parity)))
            multiply((FULL // 2, 0), (FULL // 2, 1))
            multiply((FULL // 2, 1), None)

        @block.sync
        def _(sp):
            for t, (_, s_, z_) in enumerate(quantised[:2]):
                for buf, src in ((scales[t], s_), (zeros[t], z_)):
                    sp.dma_start(buf[:, 0:FULL, :], src[0:FULL * P, :].rearrange("(c p) g -> p c g", p=P)
                                 ).then_inc(tables_loaded, 16)
                    sp.dma_start(buf[0:REST, FULL, :], src[FULL * P:, :]).then_inc(tables_loaded, 16)
            for buf, src in ((scales[DOWN], down_s), (zeros[DOWN], down_z)):
                sp.dma_start(buf[:], src.rearrange("(k p) g -> p k g", p=P)).then_inc(tables_loaded, 16)
            for s in range(2):
                sp.sem_inc(hi_stored[s], 16)
                sp.sem_inc(lo_stored[s], 16)

            def prepare(chunk, kind):
                m, slot = weights(chunk, kind)
                n, c = height(chunk), number(chunk)
                rows, packed = extent(kind, chunk)
                wait_positive(sp, unpacked, m - 1)
                if kind == DOWN:
                    dst = RAW[:, slot, 0:packed].rearrange("p (k i) -> p k i", k=KC)
                    src = down_q[:, bass.ds(c * (P // 2), n // 2)].rearrange("(k p) i -> p k i", p=P)
                else:
                    dst, src = RAW[0:n, slot, :], (gate_q, up_q)[kind][bass.ds(c * P, n), :]
                sp.dma_start(dst, src).then_inc(raw_loaded[slot], 16)

            def multiply(chunk, coming):
                c, n = number(chunk), height(chunk)
                for b in range(NB):
                    if coming and b < 3:
                        prepare(coming, b)
                    for buf, done, dram, stored in ((HH, hi_done, h_hi, hi_stored), (HL, lo_done, h_lo, lo_stored)):
                        sp.wait_ge(done, NB * c + b + 1 + (FREE if done is lo_done else 0))
                        sp.dma_start(dram[bass.ds(c * P, n), b * BANK:(b + 1) * BANK], buf[0:n, b % 2, :]
                                     ).then_inc(stored[b % 2], 16)
            all_chunks(sp, prepare, multiply)
            for s in range(2):
                sp.wait_ge(hi_stored[s], 16 * (NB // 2 * CHUNKS + 1))
                sp.wait_ge(lo_stored[s], 16 * (NB // 2 * CHUNKS + 1))

        @block.tensor
        def _(pe):
            def prepare(chunk, kind):
                m, slot = weights(chunk, kind)
                n = height(chunk)
                wait_positive(pe, cut_lo, m - 1)
                pe.wait_ge(scaled, m + 1)
                for k in range(KC):
                    if kind == DOWN:
                        last = nc.tensor.transpose(WT[0:n, slot, k * P:(k + 1) * P], W[:, slot, k * n:(k + 1) * n],
                                                   ident[:])
                    else:
                        last = nc.tensor.transpose(WT[:, slot, k * P:k * P + n], W[0:n, slot, k * P:(k + 1) * P],
                                                   ident[0:n, 0:n])
                last.then_inc(turned, 1)

            def multiply(chunk, coming):
                c, n, parity = number(chunk), height(chunk), chunk[1]
                for b in range(NB):
                    if b == 0:
                        pe.wait_ge(cut_lo, 6 * chunk[0] + 3 * parity + 2)
                    pe.wait_ge(h_done, NB * c + b - 1 + FREE)
                    tok = slice(b * BANK, (b + 1) * BANK)
                    for kind, out, done in ((GATE, GP, gate_product), (UP, UP_, up_product)):
                        o = out[0:n, b % 2, :]
                        for k in range(KC):
                            wh, wl = (w[:, kind, parity, k, 0:n] for w in (w_hi, w_lo))
                            nc.tensor.matmul(o, wh, x2_hi[:, k, tok], start=(k == 0), stop=False)
                            nc.tensor.matmul(o, wh, x2_lo[:, k, tok], start=False, stop=False)
                            last = nc.tensor.matmul(o, wl, x2_hi[:, k, tok], start=False, stop=(k == KC - 1))
                        last.then_inc(done, 1)
                    if coming and b < 3:
                        prepare(coming, b)
            all_chunks(pe, prepare, multiply)

        @block.vector
        def _(dve):
            dve.sem_inc(h_done, FREE)
            dve.wait_ge(tables_loaded, 16 * 10)

            def unpack(chunk, kind):
                m, slot = weights(chunk, kind)
                rows, packed = extent(kind, chunk)
                wait_positive(dve, shifted, m)
                dve.wait_ge(raw_loaded[slot], 16 * (3 * chunk[0] + (3 * chunk[1] + kind) // 2 + 1))
                raw = RAW[0:rows, slot, 0:packed]
                pair = NIBBLES[0:rows, 0:2 * packed].rearrange("p (j two) -> p two j", two=2)
                nc.vector.tensor_scalar(pair[:, 0, :], raw, 4, 15, ALU.logical_shift_right, ALU.bitwise_and)
                nc.vector.tensor_scalar(pair[:, 1, :], raw, 15, None, ALU.bitwise_and).then_inc(unpacked, 1)
                wait_positive(dve, turned, m - 1)
                dve.wait_ge(unpacked, m + 1)
                nc.vector.tensor_tensor(grouped(W[:, slot], kind, chunk), grouped(NIBBLES, kind, chunk),
                                        table(zeros, kind, chunk), ALU.subtract).then_inc(shifted, 1)

            def cut(chunk, kind):
                m, _ = weights(chunk, kind)
                psum, hi, lo = turned_parts(kind, chunk)
                dve.wait_ge(cut_hi, m + 1)
                nc.vector.scalar_tensor_tensor(lo, psum, WS, hi, ALU.mult, ALU.subtract).then_inc(cut_lo, 1)

            def prepare(chunk, kind):
                unpack(chunk, kind)
                cut(chunk, kind)

            def multiply(chunk, coming):
                c, n = number(chunk), height(chunk)
                for b in range(NB):
                    if coming and b < 3:
                        unpack(coming, b)
                    dve.wait_ge(lo_done, NB * c + b - 1 + FREE)
                    dve.wait_ge(silu_done, NB * c + b + 1)
                    dve.wait_ge(up_product, NB * c + b + 1)
                    nc.vector.scalar_tensor_tensor(H[0:n, b % 2, :], UP_[0:n, b % 2, :], HS * in_scale,
                                                   SILU[0:n, b % 2, :], ALU.mult, ALU.mult).then_inc(h_done, 1)
                    if coming and b < 3:
                        cut(coming, b)
            all_chunks(dve, prepare, multiply)

        @block.scalar
        def _(act):
            def prepare(chunk, kind):
                m, _ = weights(chunk, kind)
                psum, hi, lo = turned_parts(kind, chunk)
                act.wait_ge(turned, m + 1)
                nc.scalar.activation(hi, psum, ACT.Copy, scale=WS).then_inc(cut_hi, 1)

            def multiply(chunk, coming):
                c, n = number(chunk), height(chunk)
                for b in range(NB):
                    act.wait_ge(gate_product, NB * c + b + 1)
                    nc.scalar.activation(SILU[0:n, b % 2, :], GP[0:n, b % 2, :], ACT.Silu, scale=in_scale
                                         ).then_inc(silu_done, 1)
                    act.wait_ge(hi_stored[b % 2], 16 * (NB // 2 * c + b // 2 + 1))
                    act.wait_ge(lo_done, NB * c + b - 1 + FREE)
                    act.wait_ge(h_done, NB * c + b + 1 + FREE)
                    nc.scalar.activation(HH[0:n, b % 2, :], H[0:n, b % 2, :], ACT.Copy).then_inc(hi_done, 1)
                    if coming and b < 3:
                        prepare(coming, b)
            all_chunks(act, prepare, multiply)

        @block.gpsimd
        def _(pool):
            pool.sem_inc(lo_done, FREE)
            for w in (wd_hi, wd_lo):
                last = nc.gpsimd.memset(w[REST:P, FULL, :], 0.0)
            last.then_inc(cleared, 1)
            pool.wait_ge(cleared, 1)
            pool.wait_ge(tables_loaded, 16 * 10)

            def prepare(chunk, kind):
                m, slot = weights(chunk, kind)
                pool.wait_ge(shifted, m + 1)
                nc.gpsimd.tensor_tensor(grouped(W[:, slot], kind, chunk), grouped(W[:, slot], kind, chunk),
                                        table(scales, kind, chunk), ALU.mult).then_inc(scaled, 1)

            def multiply(chunk, coming):
                c, n = number(chunk), height(chunk)
                for b in range(NB):
                    if coming and b < 3:
                        prepare(coming, b)
                    pool.wait_ge(lo_stored[b % 2], 16 * (NB // 2 * c + b // 2 + 1))
                    pool.wait_ge(hi_done, NB * c + b + 1)
                    nc.gpsimd.tensor_tensor(HL[0:n, b % 2, :], H[0:n, b % 2, :], HH[0:n, b % 2, :], ALU.subtract
                                            ).then_inc(lo_done, 1)
            all_chunks(pool, prepare, multiply)


def project_down(nc, h_hi, h_lo, wd_hi, wd_lo, x1_dram, out, sem):
    CHUNKS, D = wd_hi.shape[1], wd_hi.shape[2]
    inter, T = h_hi.shape
    FULL, REST = inter // P, inter % P
    BLOCK = 2 * P
    ROUNDS = T // BLOCK // 2
    h_loaded = [sem(f"f_h_loaded{u}") for u in range(2)]
    x_loaded = [sem(f"f_x_loaded{u}") for u in range(2)]
    stored = [sem(f"f_stored{u}") for u in range(2)]
    product, normed, added, cleared = sem("f_product"), sem("f_normed"), sem("f_added"), sem("f_cleared")
    with ExitStack() as ctx:
        sb = lambda n, s, d=F32: ctx.enter_context(nc.sbuf_tensor("f_" + n, s, d))
        H_HI, H_LO = (sb(n, [P, 2, CHUNKS, BLOCK], F16) for n in ("h_hi", "h_lo"))
        X = sb("x", [P, 2, 2, D])
        Z = sb("z", [P, 2, 2, D])
        norm = RowNorm(nc, ctx, sem, "f_norm", HS * WS, 1.0)
        YP = ctx.enter_context(nc.psum_tensor("f_yp", [P, 2, 2, D], F32))
        block = ctx.enter_context(nc.Block())

        def rows(i, u):
            return bass.ds((2 * i + u) * BLOCK, BLOCK)

        @block.sync
        def _(sp):
            def load(i, u):
                for buf, src in ((H_HI, h_hi), (H_LO, h_lo)):
                    sp.dma_start(buf[:, u, 0:FULL, :], src[0:FULL * P, rows(i, u)].rearrange("(c p) t -> p c t", p=P)
                                 ).then_inc(h_loaded[u], 16)
                    sp.dma_start(buf[0:REST, u, FULL, :], src[FULL * P:, rows(i, u)]).then_inc(h_loaded[u], 16)
                sp.dma_start(X[:, u], x1_dram[rows(i, u), :].rearrange("(s p) d -> p s d", p=P)
                             ).then_inc(x_loaded[u], 16)

            def store(i, u):
                sp.wait_ge(added, 4 * i + 2 * u + 2)
                sp.dma_start(out[rows(i, u), :].rearrange("(s p) d -> p s d", p=P), Z[:, u]).then_inc(stored[u], 16)
            load(0, 0)
            load(0, 1)
            with sp.Fori(0, ROUNDS - 1) as i:
                for u in range(2):
                    store(i, u)
                    load(i + 1, u)
            for u in range(2):
                store(ROUNDS - 1, u)
            for u in range(2):
                sp.wait_ge(stored[u], 16 * ROUNDS)

        @block.tensor
        def _(pe):
            pe.wait_ge(cleared, 1)

            def block_product(i, u, first):
                pe.wait_ge(h_loaded[u], 64 * i + 64)
                for s in range(2):
                    if not first:
                        pe.wait_ge(normed, 4 * i + 2 * u + s - 3)
                    for c in range(CHUNKS):
                        hh, hl = (h[:, u, c, s * P:(s + 1) * P] for h in (H_HI, H_LO))
                        for stat, w, a, z in ((hh, wd_hi, 1, 0), (hh, wd_lo, 0, 0), (hl, wd_hi, 0, 1)):
                            for n in range(0, D, BANK):
                                last = nc.tensor.matmul(YP[:, u, s, n:n + BANK], stat, w[:, c, n:n + BANK],
                                                        start=(c == 0 and a == 1), stop=(c == CHUNKS - 1 and z == 1))
                    last.then_inc(product, 1)
            block_product(0, 0, True)
            block_product(0, 1, True)
            with pe.Fori(1, ROUNDS) as i:
                for u in range(2):
                    block_product(i, u, False)

        @block.vector
        def _(dve):
            def normalise(i, u, first):
                if not first:
                    dve.wait_ge(stored[u], 16 * i)
                norm.on_vector(dve, 2 * i + u, lambda s: dve.wait_ge(product, 4 * i + 2 * u + s + 1),
                               lambda s: YP[:, u, s, :], lambda s: Z[:, u, s, :], normed)
            normalise(0, 0, True)
            normalise(0, 1, True)
            with dve.Fori(1, ROUNDS) as i:
                for u in range(2):
                    normalise(i, u, False)

        @block.scalar
        def _(act):
            with act.Fori(0, 2 * ROUNDS) as r:
                norm.on_scalar(act, r)

        @block.gpsimd
        def _(pool):
            for h in (H_HI, H_LO):
                last = nc.gpsimd.memset(h[REST:P, :, FULL, :], 0.0)
            last.then_inc(cleared, 1)
            pool.wait_ge(cleared, 1)
            with pool.Fori(0, ROUNDS) as i:
                for u in range(2):
                    pool.wait_ge(x_loaded[u], 16 * i + 16)
                    for s in range(2):
                        pool.wait_ge(normed, 4 * i + 2 * u + s + 1)
                        nc.gpsimd.tensor_tensor(Z[:, u, s, :], X[:, u, s, :], Z[:, u, s, :], ALU.add
                                                ).then_inc(added, 1)


def sandwich_layer(nc, x, wq, wkv, wo, bo, gate_q, up_q, down_q, gate_s, gate_z, up_s, up_z,
                   down_s, down_z, out, debug=None):
    T, D = x.shape
    NT, KC = T // P, D // P
    VC = wkv.shape[1] // 2
    QK = D + VC
    inter = gate_q.shape[0]
    qk_hi, qk_lo = (nc.dram_tensor(n, (QK, T), F16).ap() for n in ("qk_hi", "qk_lo"))
    h_hi, h_lo = (nc.dram_tensor(n, (inter, T), F16).ap() for n in ("h_hi", "h_lo"))
    x1_dram = nc.dram_tensor("x1_dram", (T, D), F32).ap()
    with ExitStack() as whole:
        def sem(name):
            return whole.enter_context(nc.semaphore(name))

        def tensor(stack, name, shape, dtype, side="left"):
            return stack.enter_context(nc.sbuf_tensor(name, shape, dtype, side=side))
        ident, identb = tensor(whole, "ident", [P, P], F32), tensor(whole, "identb", [P, P], BF16)
        causal, ones = tensor(whole, "causal", [P, P], BF16), tensor(whole, "ones", [P, D // HEADS], F32)
        build_constants(nc, ident, identb, causal, ones, sem)
        with ExitStack() as context:
            c_hi, c_lo = (tensor(context, n, [P, KC, T], F16) for n in ("c_hi", "c_lo"))
            with ExitStack() as attention:
                v_sb = tensor(attention, "v_sb", [P, NT, VC], F32, "right")
                with ExitStack() as stage:
                    w_hi, w_lo = (tensor(stage, n, [P, KC, QK + VC], F16) for n in ("w_hi", "w_lo"))
                    normalise_and_load_weights(nc, x, wq, wkv, ident, c_hi, c_lo, w_hi, w_lo, sem)
                    project_qkv(nc, c_hi, c_lo, w_hi, w_lo, qk_hi, qk_lo, v_sb, sem)
                if debug == "qkv":
                    return
                attend(nc, qk_hi, qk_lo, v_sb, ident, identb, causal, ones, c_hi, c_lo, sem)
            if debug == "attn":
                dbg = nc.dram_tensor("ctx_dbg", (D, T), F32).ap()
                n = sem("dbg")
                with nc.Block() as block:
                    @block.gpsimd
                    def _(e):
                        e.dma_start(dbg.rearrange("(c p) t -> p c t", p=P), c_hi[:]).then_inc(n, 16)
                        e.wait_ge(n, 16)
                return
            ffn = whole.enter_context(ExitStack())
            x2_hi, x2_lo = (tensor(ffn, n, [P, KC, T], F16, "right") for n in ("x2_hi", "x2_lo"))
            project_context(nc, c_hi, c_lo, wo, bo, x, x1_dram, ident, x2_hi, x2_lo, sem)
        if debug == "x1":
            return
        wd_hi, wd_lo = (tensor(whole, n, [P, -(-inter // P), D], F16) for n in ("wd_hi", "wd_lo"))
        gate_and_up(nc, x2_hi, x2_lo, ((gate_q, gate_s, gate_z), (up_q, up_s, up_z), (down_q, down_s, down_z)),
                    ident, wd_hi, wd_lo, h_hi, h_lo, sem)
        ffn.close()
        project_down(nc, h_hi, h_lo, wd_hi, wd_lo, x1_dram, out, sem)


INPUTS = ["L0_attn_x", "L0_attn_Wq", "L0_attn_Wkv", "L0_attn_Wo", "L0_attn_bo", "L0_ffn_gate_Wq", "L0_ffn_up_Wq",
          "L0_ffn_down_Wq", "L0_ffn_gate_scale", "L0_ffn_gate_zero", "L0_ffn_up_scale", "L0_ffn_up_zero",
          "L0_ffn_down_scale", "L0_ffn_down_zero"]


def kernel(**inputs):
    import numpy as np
    from concourse import bacc
    from concourse.bass_utils import run_bass_kernel_spmd

    nc = bacc.Bacc("TRN2", target_bir_lowering=False, num_devices=1)
    arrays, args = {}, []
    shape = np.shape(inputs["L0_attn_x"])
    for name in INPUTS:
        a = np.ascontiguousarray(inputs[name])
        if name == "L0_attn_x":
            a = a.reshape(shape[1:])
        arrays[name] = a
        args.append(nc.dram_tensor(name, a.shape, mybir.dt.from_np(a.dtype), kind="ExternalInput").ap())
    args.append(nc.dram_tensor("out", shape[1:], F32, kind="ExternalOutput").ap())
    sandwich_layer(nc, *args)
    result = run_bass_kernel_spmd(nc, [arrays], core_ids=[0])
    return result.results[0]["out"].reshape(shape)
```

```python
from contextlib import ExitStack

import concourse.bass as bass
from concourse import mybir

P = 128
BANK = 512
F32, F16, BF16, I32 = mybir.dt.float32, mybir.dt.float16, mybir.dt.bfloat16, mybir.dt.int32
ALU = mybir.AluOpType
ACT = mybir.ActivationFunctionType
AX = mybir.AxisListType

EPS = 1e-5
HEADS, GROUPS = 32, 8
QGROUP = 64
XS = 16.0
WS = 1024.0
QS = 16.0
CS = 64.0
HS = 16.0
MS = QS * QS
MASKED = -1.0e30
LEAST = -3.0e38


def build_constants(nc, ident, identb, causal, ones, sem):
    zeroed, made = sem("consts_zeroed"), sem("consts_made")
    with nc.Block() as block:
        @block.gpsimd
        def _(pool):
            nc.gpsimd.memset(ident[:], 0.0)
            nc.gpsimd.memset(identb[:], 0.0)
            nc.gpsimd.memset(ones[:], 1.0)
            nc.gpsimd.memset(causal[:], 0.0).then_inc(zeroed, 1)
            pool.wait_ge(zeroed, 1)
            for m in (ident, identb):
                nc.gpsimd.affine_select(out=m[:], in_=m[:], compare_op=ALU.not_equal, fill=1.0, base=0,
                                        pattern=[[-1, P]], channel_multiplier=1)
            nc.gpsimd.affine_select(out=causal[:], in_=causal[:], compare_op=ALU.is_ge, fill=MASKED, base=0,
                                    pattern=[[-1, P]], channel_multiplier=1).then_inc(made, 1)


class RowNorm:

    def __init__(self, nc, ctx, sem, name, in_scale, out_scale):
        self.nc = nc
        self.keep, self.root_scale = in_scale ** -2, (in_scale / out_scale) ** 2
        sb = lambda n, s: ctx.enter_context(nc.sbuf_tensor(f"{name}_{n}", s, F32))
        self.stats, self.mv = sb("stats", [P, 2, 2, 6]), sb("mv", [P, 2, 2])
        self.var, self.root, self.rstd = sb("var", [P, 2]), sb("root", [P, 2]), sb("rstd", [P, 2])
        self.stats_done, self.stats_seen, self.aggr_done, self.var_done, self.root_done, self.rstd_done = (
            sem(f"{name}_{n}") for n in
            ("stats_done", "stats_seen", "aggr_done", "var_done", "root_done", "rstd_done"))

    def on_vector(self, dve, r, wait_source, source, target, done):
        nc = self.nc
        for s in range(2):
            wait_source(s)
            rows = source(s)
            half = rows.shape[-1] // 2
            nc.vector.bn_stats(self.stats[:, s, 0, :], rows[:, 0:half])
            nc.vector.bn_stats(self.stats[:, s, 1, :], rows[:, half:]).then_inc(self.stats_done, 1)
        dve.wait_ge(self.stats_done, 2 * r + 2)
        dve.sem_inc(self.stats_seen, 1)
        for s in range(2):
            nc.vector.bn_aggr(self.mv[:, s, :], self.stats[:, s, :, :]).then_inc(self.aggr_done, 1)
        dve.wait_ge(self.aggr_done, 2 * r + 2)
        nc.vector.tensor_scalar(self.var[:], self.mv[:, :, 1], self.keep, EPS, ALU.mult, ALU.add
                                ).then_inc(self.var_done, 1)
        dve.wait_ge(self.root_done, r + 1)
        nc.vector.reciprocal(self.rstd[:], self.root[:]).then_inc(self.rstd_done, 1)
        dve.wait_ge(self.rstd_done, r + 1)
        for s in range(2):
            nc.vector.tensor_scalar(target(s), source(s), self.mv[:, s, 0:1], self.rstd[:, s:s + 1],
                                    ALU.subtract, ALU.mult).then_inc(done, 1)

    def on_scalar(self, act, r):
        act.wait_ge(self.var_done, r + 1)
        self.nc.scalar.activation(self.root[:], self.var[:], ACT.Sqrt, scale=self.root_scale
                                  ).then_inc(self.root_done, 1)


def project_qkv(nc, x, wq, wkv, ident, x_hi, x_lo, w_hi, w_lo, qk_hi, qk_lo, v_sb, sem):
    T, D = x.shape
    KC = D // P
    QK = qk_hi.shape[0]
    NB, TILES, COLS = T // BANK, BANK // P, QK // P
    VC = v_sb.shape[2]
    RING = 5
    WBUF = 4
    assert COLS == 2 * RING and TILES == RING - 1 and KC % WBUF == 0
    TURN_AFTER = {2: 0, 4: 1, 7: 2, 8: 3}
    NORM_AFTER = {0: 0, 4: 1}
    x_loaded = [sem(f"b_x_loaded{s}") for s in range(TILES)]
    w_loaded = [sem(f"b_w_loaded{s}") for s in range(WBUF)]
    w_cut_hi, w_cut_lo = sem("b_w_cut_hi"), sem("b_w_cut_lo")
    norm_done, turned, x_cut_hi, x_cut_lo = (sem("b_" + n) for n in ("norm_done", "turned", "x_cut_hi", "x_cut_lo"))
    product, hi_done, lo_done = sem("b_product"), sem("b_hi_done"), sem("b_lo_done")
    v_product, v_done = sem("b_v_product"), sem("b_v_done")
    hi_stored = [sem(f"b_hi_stored{b}") for b in range(RING)]
    lo_stored = [sem(f"b_lo_stored{b}") for b in range(RING)]
    out_scale = QS / (XS * WS)
    with ExitStack() as ctx:
        sb = lambda n, s, d=F32: ctx.enter_context(nc.sbuf_tensor("b_" + n, s, d))
        X, XN = sb("x", [P, TILES, D]), sb("xn", [P, TILES, D])
        W = sb("w", [P, WBUF, D + 2 * VC])
        HI, LO = sb("hi", [P, RING, BANK], F16), sb("lo", [P, RING, BANK], F16)
        norm = RowNorm(nc, ctx, sem, "b_norm", 1.0, XS)
        XT = ctx.enter_context(nc.psum_tensor("b_xt", [P, KC * P], F32))
        PS = ctx.enter_context(nc.psum_tensor("b_ps", [P, RING, BANK], F32))
        block = ctx.enter_context(nc.Block())

        def of_kind(ap, kind):
            return ap.rearrange("p (g two d) -> p two g d", two=2, g=GROUPS)[:, kind]

        def columns(w, i, kind):
            at = D + kind * VC
            return w[:, i, at:at + VC].rearrange("p (g d) -> p g d", g=GROUPS)

        def tile(x, b, s):
            return x[:, :, bass.ds((TILES * b + s) * P, P)]

        def all_blocks(eng, body):
            body(0, first=True, last=False)
            with eng.Fori(1, NB - 1) as b:
                body(b, first=False, last=False)
            body(NB - 1, first=False, last=True)

        @block.sync
        def _(sp):
            def load_tile(b, s):
                sp.dma_start(X[:, s, :], x[bass.ds((TILES * b + s) * P, P), :]).then_inc(x_loaded[s], 16)

            def body(b, first, last):
                if not last:
                    for s in range(TILES):
                        sp.wait_ge(norm_done, TILES * b + s + 1)
                        load_tile(b + 1, s)
                for c in range(COLS):
                    r = c % RING
                    sp.wait_ge(hi_done, COLS * b + c + 1)
                    sp.dma_start(qk_hi[c * P:(c + 1) * P, bass.ds(b * BANK, BANK)], HI[:, r, :]
                                 ).then_inc(hi_stored[r], 16)
                    sp.wait_ge(lo_done, COLS * b + c + 1)
                    sp.dma_start(qk_lo[c * P:(c + 1) * P, bass.ds(b * BANK, BANK)], LO[:, r, :]
                                 ).then_inc(lo_stored[r], 16)
            for s in range(TILES):
                load_tile(0, s)
            for i in range(KC):
                if i >= WBUF:
                    sp.wait_ge(w_cut_lo, 3 * (i - WBUF) + 3)
                sp.dma_start(W[:, i % WBUF, 0:D], wq[i * P:(i + 1) * P, :]).then_inc(w_loaded[i % WBUF], 16)
                sp.dma_start(W[:, i % WBUF, D:], wkv[i * P:(i + 1) * P, :]).then_inc(w_loaded[i % WBUF], 16)
            all_blocks(sp, body)
            for r in range(RING):
                sp.wait_ge(hi_stored[r], 16 * 2 * NB)
                sp.wait_ge(lo_stored[r], 16 * 2 * NB)

        @block.tensor
        def _(pe):
            def turn(b, s, first=False):
                pe.wait_ge(norm_done, TILES * b + s + 1)
                if not first:
                    pe.wait_ge(x_cut_lo, TILES * b + s)
                for c in range(KC):
                    last = nc.tensor.transpose(XT[:, c * P:(c + 1) * P], XN[:, s, c * P:(c + 1) * P], ident[:])
                last.then_inc(turned, 1)

            def column_chunk(b, c, k):
                wh, wl = (w[:, k, c * P:(c + 1) * P] for w in (w_hi, w_lo))
                xh, xl = (x[:, k, bass.ds(b * BANK, BANK)] for x in (x_hi, x_lo))
                o = PS[:, c % RING, :]
                nc.tensor.matmul(o, wh, xh, start=(k == 0), stop=False)
                nc.tensor.matmul(o, wh, xl, start=False, stop=False)
                return nc.tensor.matmul(o, wl, xh, start=False, stop=(k == KC - 1))

            def value_tile(b, u):
                pe.wait_ge(lo_done, COLS * b + RING + u + 1)
                for k in range(KC):
                    xh, xl = (x[:, k, bass.ds((TILES * b + u) * P, P)] for x in (x_hi, x_lo))
                    wh, wl = w_hi[:, k, QK:QK + VC], w_lo[:, k, QK:QK + VC]
                    o = PS[:, u, 0:VC]
                    nc.tensor.matmul(o, xh, wh, start=(k == 0), stop=False)
                    nc.tensor.matmul(o, xh, wl, start=False, stop=False)
                    last = nc.tensor.matmul(o, xl, wh, start=False, stop=(k == KC - 1))
                last.then_inc(v_product, 1)

            def body(b, first, last):
                pe.wait_ge(x_cut_lo, TILES * b + TILES)
                if first:
                    for k in range(KC):
                        pe.wait_ge(w_cut_lo, 3 * k + 3)
                        for c in range(RING):
                            done = column_chunk(b, c, k)
                            if k == KC - 1:
                                done.then_inc(product, 1)
                for c in range(COLS):
                    if not (first and c < RING):
                        if c < TILES:
                            pe.wait_ge(v_done, TILES * b + c + 1 - TILES)
                        else:
                            pe.wait_ge(lo_done, COLS * b + c + 1 - RING)
                        for k in range(KC):
                            done = column_chunk(b, c, k)
                        done.then_inc(product, 1)
                    if c in TURN_AFTER and not last:
                        turn(b + 1, TURN_AFTER[c])
                for u in range(TILES):
                    value_tile(b, u)
            for s in range(TILES):
                turn(0, s, s == 0)
            all_blocks(pe, body)

        @block.scalar
        def _(act):
            def cut_tile(b, s):
                act.wait_ge(turned, TILES * b + s + 1)
                nc.scalar.activation(tile(x_hi, b, s), XT[:].rearrange("p (c t) -> p c t", t=P), ACT.Copy
                                     ).then_inc(x_cut_hi, 1)

            def body(b, first, last):
                for c in range(COLS):
                    if not (first and c < RING):
                        act.wait_ge(hi_stored[c % RING], 16 * (2 * b + c // RING))
                    act.wait_ge(product, COLS * b + c + 1)
                    nc.scalar.activation(HI[:, c % RING, :], PS[:, c % RING, :], ACT.Copy, scale=out_scale
                                         ).then_inc(hi_done, 1)
                    if not last:
                        if c in NORM_AFTER:
                            norm.on_scalar(act, 2 * (b + 1) + NORM_AFTER[c])
                        if c in TURN_AFTER:
                            cut_tile(b + 1, TURN_AFTER[c])
            for pair in range(2):
                norm.on_scalar(act, pair)
                for s in (2 * pair, 2 * pair + 1):
                    cut_tile(0, s)
            for i in range(KC):
                act.wait_ge(w_loaded[i % WBUF], 32 * (i // WBUF) + 32)
                nc.scalar.activation(w_hi[:, i, 0:D], W[:, i % WBUF, 0:D], ACT.Copy, scale=WS).then_inc(w_cut_hi, 1)
                for kind in range(2):
                    nc.scalar.activation(columns(w_hi, i, kind), of_kind(W[:, i % WBUF, D:], kind),
                                         ACT.Copy, scale=WS).then_inc(w_cut_hi, 1)
            all_blocks(act, body)

        @block.vector
        def _(dve):
            def normalise_pair(b, pair):
                at = 2 * pair
                norm.on_vector(dve, 2 * b + pair, lambda s: dve.wait_ge(x_loaded[at + s], 16 * b + 16),
                               lambda s: X[:, at + s, :], lambda s: XN[:, at + s, :], norm_done)

            def cut_tile(b, s):
                dve.wait_ge(x_cut_hi, TILES * b + s + 1)
                nc.vector.tensor_tensor(tile(x_lo, b, s), XT[:].rearrange("p (c t) -> p c t", t=P),
                                        tile(x_hi, b, s), ALU.subtract).then_inc(x_cut_lo, 1)

            def body(b, first, last):
                for c in range(COLS):
                    if not (first and c < RING):
                        dve.wait_ge(lo_stored[c % RING], 16 * (2 * b + c // RING))
                    dve.wait_ge(hi_done, COLS * b + c + 1)
                    nc.vector.scalar_tensor_tensor(LO[:, c % RING, :], PS[:, c % RING, :], out_scale,
                                                   HI[:, c % RING, :], ALU.mult, ALU.subtract).then_inc(lo_done, 1)
                    if not last:
                        if c in NORM_AFTER:
                            normalise_pair(b + 1, NORM_AFTER[c])
                        if c in TURN_AFTER:
                            cut_tile(b + 1, TURN_AFTER[c])
                for u in range(TILES):
                    dve.wait_ge(v_product, TILES * b + u + 1)
                    nc.vector.tensor_scalar(v_sb[:, TILES * b + u, :], PS[:, u, 0:VC], 1.0 / (XS * WS), None,
                                            ALU.mult).then_inc(v_done, 1)
            for pair in range(2):
                normalise_pair(0, pair)
                for s in (2 * pair, 2 * pair + 1):
                    cut_tile(0, s)
            for i in range(KC):
                dve.wait_ge(w_cut_hi, 3 * i + 3)
                nc.vector.scalar_tensor_tensor(w_lo[:, i, 0:D], W[:, i % WBUF, 0:D], WS, w_hi[:, i, 0:D],
                                               ALU.mult, ALU.subtract).then_inc(w_cut_lo, 1)
                for kind in range(2):
                    nc.vector.scalar_tensor_tensor(
                        columns(w_lo, i, kind), of_kind(W[:, i % WBUF, D:], kind), WS, columns(w_hi, i, kind),
                        ALU.mult, ALU.subtract).then_inc(w_cut_lo, 1)
            all_blocks(dve, body)


def attend(nc, qk_hi, qk_lo, v_sb, ident, identb, causal, ones, c_hi, c_lo, sem):
    T = qk_hi.shape[1]
    D = c_hi.shape[1] * P
    HD = D // HEADS
    NT, NB, REP = T // P, T // BANK, HEADS // GROUPS
    TPB = BANK // P
    STACK = 3 * HD
    UNIT = 2 * BANK
    RING = 5
    exp_scale = float(HD) ** -0.5 / MS

    steps = [(b, k) for b in range(NB) for k in range(TPB * (b + 1))]
    STEPS = len(steps)
    last_of = {s: b for s, (b, k) in enumerate(steps) if k == TPB * (b + 1) - 1}
    assert T == 2 * UNIT
    half = NT // 2
    units = [unit for h in range(REP) for a in range(half)
             for unit in ((h, half + a, 0), (h, a, 0), (h, NT - 1 - a, 1))]
    UNITS = len(units)
    SLOTS = UNITS + 1
    width = [BANK - max(0, k - TPB * b) * P for b, k in steps]
    TURN = STEPS - 3
    share = [min(UNITS, -(-UNITS * sum(width[:s]) // sum(width[:TURN]))) for s in range(STEPS + 1)]
    units_in = [range(share[s], share[s + 1]) for s in range(STEPS)]

    sums_of_block, place_of, pairs = [], {}, []
    for b in range(NB):
        first = TPB * b * (b + 1) // 2
        last, at = first + TPB * (b + 1) - 1, 0
        for a in range(first, last, 2):
            if a + 1 == last or (b == NB - 1 and a == last - 3):
                alone = [(a, 1), (a + 1, 1)]
            else:
                alone = [(a, 2)]
                pairs.append(a)
            for first_step, count in alone:
                at = max(at, first_step + (1 if count == 1 else 4))
                place_of[first_step] = at
                sums_of_block.append((b, first_step, count))
    sum_order = sorted(sums_of_block, key=lambda e: (place_of[e[1]], e[1]))
    SUMS = len(sum_order)
    sum_of_step = {a + i: n for n, (_, a, count) in enumerate(sum_order) for i in range(count)}
    last_sum = {b: max(n for n, e in enumerate(sum_order) if e[0] == b) for b in range(NB)}
    first_sum = {b: min(n for n, e in enumerate(sum_order) if e[0] == b) for b in range(NB)}

    def sums_in(s):
        return [n for n, e in enumerate(sum_order) if place_of[e[1]] == s]

    added = sem("c_added")
    sums_done = sem("c_sums_done")
    loaded, max_stored, buffer_free = sem("c_loaded"), sem("c_max_stored"), sem("c_buffer_free")
    unit_done, maxed, max_done = sem("c_unit_done"), sem("c_maxed"), sem("c_max_done")
    scores_done, exp_done, pv_done = sem("c_scores_done"), sem("c_exp_done"), sem("c_pv_done")
    ctx_read, sum_read, normed = sem("c_ctx_read"), sem("c_sum_read"), sem("c_normed")
    inverted, values_ready = sem("c_inverted"), sem("c_values_ready")
    ctx_hi_done, ctx_lo_done, filled = sem("c_ctx_hi_done"), sem("c_ctx_lo_done"), sem("c_filled")
    S2_FREE, PROB_FREE, SUM_FREE, C_FREE, CN_FREE = 2, SUMS, 1, 2, 2

    with ExitStack() as ctx:
        sb = lambda n, s, d=F32: ctx.enter_context(nc.sbuf_tensor("c_" + n, s, d))
        ps = lambda n, s, d=F32: ctx.enter_context(nc.psum_tensor("c_" + n, s, d))
        Q, K = sb("q", [STACK + 1, 3, REP, T], F16), sb("k", [STACK + 1, 3, T], F16)
        V = sb("v", [P, NT, HD])
        PROB = sb("prob", [P, RING * REP, BANK])
        MAXES, NEGMAX = sb("maxes", [P, NT * REP, 2]), sb("negmax", [P, P])
        MROW = sb("mrow", [NT * REP, P], F16)
        C, R, CN = sb("c", [P, 2, BANK]), sb("r", [P, BANK]), sb("cn", [P, 2, BANK])
        S1 = ps("s1", [P, 2, UNIT])
        S2 = ps("s2", [P, 2, BANK])
        CTX, SUM = ps("ctx", [P, BANK]), ps("sum", [P, BANK])
        block = ctx.enter_context(nc.Block())

        def diagonal(s):
            b, k = steps[s]
            return max(0, k - TPB * b) * P, k >= TPB * b

        @block.sync
        def _(sp):
            def load_group(g, buf):
                qrows, krows = bass.ds(g * P, P), bass.ds(D + g * HD, HD)
                for row, (qs, ks) in enumerate(((qk_hi, qk_hi), (qk_lo, qk_hi), (qk_hi, qk_lo))):
                    part = slice(row * HD, (row + 1) * HD)
                    sp.dma_start(Q[part, buf], qs[qrows, :].rearrange("(h d) t -> d h t", d=HD)
                                 ).then_inc(loaded, 16)
                    sp.dma_start(K[part, buf], ks[krows, :]).then_inc(loaded, 16)

            def store_maxima(g, buf):
                sp.wait_ge(maxed, SLOTS * g + SLOTS)
                sp.dma_start(Q[STACK:STACK + 1, buf].rearrange("o h (t q) -> o (h t) q", q=P),
                             MROW[:, :]).then_inc(max_stored, 16)
            load_group(0, 0)
            sp.wait_ge(loaded, 96)
            load_group(1, 1)
            store_maxima(0, 0)
            sp.wait_ge(loaded, 192)
            load_group(2, 2)
            store_maxima(1, 1)
            with sp.Fori(1, GROUPS - 2) as g:
                sp.wait_ge(loaded, 96 * g + 192)
                sp.sem_inc(buffer_free, 1)
                sp.wait_ge(scores_done, REP * STEPS * g)
                sp.sem_inc(buffer_free, 1)
                load_group(g + 2, (g + 2) % 3)
                store_maxima(g + 1, (g + 1) % 3)
            store_maxima(GROUPS - 1, (GROUPS - 1) % 3)

        def bodies(eng, body, ahead):
            ahead()
            with eng.Fori(0, GROUPS - 1) as g:
                body(g, True)
            body(GROUPS - 1, False)

        @block.tensor
        def _(pe):
            def unit(g, n):
                h, t, u = units[n]
                buf, slot = g % 3, n % 2
                free = SLOTS * g + (n - 1 if n else 0)
                if not (isinstance(free, int) and free <= 0):
                    pe.wait_ge(maxed, free)
                end = min(UNIT, (t + 1) * P - u * UNIT)
                for c in range(0, end, BANK):
                    n_c = min(BANK, end - c)
                    diag = u * UNIT + c + n_c == (t + 1) * P
                    last = nc.tensor.matmul(S1[:, slot, c:c + n_c], Q[0:STACK, buf, h, t * P:(t + 1) * P],
                                            K[0:STACK, buf, u * UNIT + c:u * UNIT + c + n_c],
                                            start=True, stop=not diag)
                    if diag:
                        last = nc.tensor.matmul(S1[:, slot, c + n_c - P:c + n_c], identb[:], causal[:],
                                                start=False, stop=True)
                last.then_inc(unit_done, 1)

            def turn_maxima(g):
                pe.wait_ge(max_done, g + 1)
                nc.tensor.transpose(S1[:, 0, 0:P], NEGMAX[:, :], ident[:]).then_inc(unit_done, 1)

            def scores(g, s, heads):
                b, k = steps[s]
                j, diag = diagonal(s)
                buf = g % 3
                for h in heads:
                    n = REP * STEPS * g + REP * s + h
                    pe.wait_ge(exp_done, n - 1 + S2_FREE)
                    last = nc.tensor.matmul(S2[:, h % 2, j:BANK], K[:, buf, k * P:(k + 1) * P],
                                            Q[:, buf, h, b * BANK + j:(b + 1) * BANK], start=True, stop=not diag)
                    if diag:
                        last = nc.tensor.matmul(S2[:, h % 2, j:j + P], causal[:], identb[:], start=False, stop=True)
                    last.then_inc(scores_done, 1)

            def products(g, s):
                b, k = steps[s]
                j, _ = diagonal(s)
                if s == 0:
                    pe.wait_ge(values_ready, g + 1)
                pe.wait_ge(exp_done, REP * STEPS * g + REP * s + REP + S2_FREE)
                if k == 0:
                    pe.wait_ge(ctx_read, NB * g + b + SUM_FREE)
                for h in range(REP):
                    last = nc.tensor.matmul(CTX[h * HD:(h + 1) * HD, j:BANK], V[:, k, :],
                                            PROB[:, REP * (s % RING) + h, j:BANK],
                                            start=(k == 0), stop=(k == TPB * (b + 1) - 1))
                last.then_inc(pv_done, 1)

            def sums(g, place):
                for n in sums_in(place):
                    b, s, count = sum_order[n]
                    j, _ = diagonal(s)
                    if n == first_sum[b]:
                        pe.wait_ge(sum_read, NB * g + b + SUM_FREE)
                    if count == 2:
                        pe.wait_ge(added, len(pairs) * g + pairs.index(s) + 1)
                    for h in range(REP):
                        last = nc.tensor.matmul(SUM[h * HD:(h + 1) * HD, j:BANK], ones[:],
                                                PROB[:, REP * (s % RING) + h, j:BANK],
                                                start=(n == first_sum[b]), stop=(n == last_sum[b]))
                    last.then_inc(sums_done, 1)

            def ahead():
                pe.sem_inc(sums_done, PROB_FREE)
                pe.wait_ge(loaded, 96)
                for n in range(UNITS):
                    unit(0, n)
                turn_maxima(0)

            def body(g, first_pass):
                pe.wait_ge(max_stored, 16 * g + 16)
                if first_pass:
                    pe.wait_ge(loaded, 96 * g + 192)

                def some_units(s, third):
                    if first_pass:
                        n = units_in[s]
                        for i in n[len(n) * third // 3:len(n) * (third + 1) // 3]:
                            unit(g + 1, i)
                for s in range(STEPS):
                    scores(g, s, (0, 1))
                    some_units(s, 0)
                    if s:
                        products(g, s - 1)
                    some_units(s, 1)
                    scores(g, s, (2, 3))
                    sums(g, s)
                    some_units(s, 2)
                    if first_pass and s == TURN:
                        turn_maxima(g + 1)
                products(g, STEPS - 1)
                sums(g, STEPS)
            bodies(pe, body, ahead)

        @block.scalar
        def _(act):
            act.sem_inc(exp_done, S2_FREE)
            act.sem_inc(ctx_read, SUM_FREE)

            def read_context(g, b, s):
                act.wait_ge(pv_done, STEPS * g + s + 1)
                act.wait_ge(normed, NB * g + b - 1 + C_FREE)
                nc.scalar.activation(C[:, b % 2, :], CTX[:, :], ACT.Copy, scale=CS).then_inc(ctx_read, 1)
            with act.Fori(0, GROUPS) as g:
                for s in range(STEPS):
                    j, _ = diagonal(s)
                    before = sum_of_step[s - RING] + SUMS if s >= RING else sum_of_step[s - RING + STEPS]
                    act.wait_ge(sums_done, SUMS * g + before + 1)
                    for h in range(REP):
                        act.wait_ge(scores_done, REP * STEPS * g + REP * s + h + 1)
                        nc.scalar.activation(PROB[:, REP * (s % RING) + h, j:BANK], S2[:, h % 2, j:BANK], ACT.Exp,
                                             scale=exp_scale).then_inc(exp_done, 1)
                    if s - 1 in last_of:
                        read_context(g, last_of[s - 1], s - 1)
                read_context(g, NB - 1, STEPS - 1)

        @block.vector
        def _(dve):
            def unit(g, n):
                h, t, u = units[n]
                end = min(UNIT, (t + 1) * P - u * UNIT)
                dve.wait_ge(unit_done, SLOTS * g + n + 1)
                nc.vector.tensor_reduce(MAXES[:, h * NT + t, u:u + 1], S1[:, n % 2, 0:end],
                                        AX.X, ALU.max).then_inc(maxed, 1)

            def join_maxima(g):
                dve.wait_ge(maxed, SLOTS * g + UNITS)
                nc.vector.tensor_reduce(NEGMAX[:, 0:NT * REP], MAXES[:, :, :], AX.X, ALU.max, negate=True
                                        ).then_inc(max_done, 1)

            def write_maxima(g):
                if not (isinstance(g, int) and g == 0):
                    dve.wait_ge(max_stored, 16 * g)
                dve.wait_ge(unit_done, SLOTS * g + SLOTS)
                nc.vector.tensor_scalar(MROW[:, :], S1[0:NT * REP, 0, 0:P], 1.0 / MS, None, ALU.mult
                                        ).then_inc(maxed, 1)

            def ahead():
                dve.sem_inc(sum_read, SUM_FREE)
                dve.sem_inc(normed, C_FREE)
                nc.vector.memset(MAXES[:], LEAST)
                nc.vector.memset(NEGMAX[:], 0.0)
                nc.vector.memset(K[STACK:STACK + 1, :, :], MS).then_inc(filled, 1)
                dve.wait_ge(filled, 1)
                for n in range(UNITS):
                    unit(0, n)
                join_maxima(0)
                write_maxima(0)

            PIECES = 4
            piece = BANK // PIECES

            def invert_piece(g, b, i):
                n = NB * g + b
                if i == 0:
                    dve.wait_ge(sums_done, SUMS * g + last_sum[b] + 1 + PROB_FREE)
                    dve.wait_ge(normed, n + C_FREE)
                at = slice(i * piece, (i + 1) * piece)
                last = nc.vector.reciprocal(R[:, at], SUM[:, at])
                if i == PIECES - 1:
                    last.then_inc(sum_read, 1)

            def normalise(g, b):
                n = NB * g + b
                dve.wait_ge(ctx_lo_done, n - 1 + CN_FREE)
                dve.wait_ge(ctx_read, n + 1 + SUM_FREE)
                dve.wait_ge(sum_read, n + 1 + SUM_FREE)
                nc.vector.tensor_tensor(CN[:, b % 2, :], C[:, b % 2, :], R[:], ALU.mult).then_inc(normed, 1)

            def body(g, first_pass, first_group):
                left = [] if first_group else [(g - 1, NB - 1, i) for i in range(PIECES + 1)]

                def one_piece():
                    if left:
                        of, b, i = left.pop(0)
                        if i < PIECES:
                            invert_piece(of, b, i)
                        else:
                            normalise(of, b)
                if first_pass:
                    dve.wait_ge(max_done, g + 1)
                for s in range(STEPS):
                    if s - 2 in last_of:
                        left += [(g, last_of[s - 2], i) for i in range(PIECES + 1)]
                    one_piece()
                    if first_pass:
                        for n in units_in[s]:
                            unit(g + 1, n)
                            if n == UNITS - 1:
                                join_maxima(g + 1)
                        if s == TURN:
                            write_maxima(g + 1)
                assert not left
            ahead()
            body(0, True, True)
            with dve.Fori(1, GROUPS - 1) as g:
                body(g, True, False)
            body(GROUPS - 1, False, False)
            for i in range(PIECES):
                invert_piece(GROUPS - 1, NB - 1, i)
            normalise(GROUPS - 1, NB - 1)

        @block.gpsimd
        def _(pool):
            def take_values(g):
                nc.gpsimd.tensor_copy(V[:, :, :], v_sb[:, :, bass.ds(g * HD, HD)]).then_inc(values_ready, 1)

            def cut_context(g, b):
                n = NB * g + b
                at = slice(b * BANK, (b + 1) * BANK)
                pool.wait_ge(normed, n + 1 + C_FREE)
                nc.gpsimd.tensor_copy(c_hi[:, g, at], CN[:, b % 2, :]).then_inc(ctx_hi_done, 1)
                pool.wait_ge(ctx_hi_done, n + 1)
                nc.gpsimd.tensor_tensor(c_lo[:, g, at], CN[:, b % 2, :], c_hi[:, g, at], ALU.subtract
                                        ).then_inc(ctx_lo_done, 1)
            def add_pair(g, n):
                a = pairs[n]
                j, _ = diagonal(a + 1)
                pool.wait_ge(pv_done, STEPS * g + a + 1)
                pool.wait_ge(exp_done, REP * (STEPS * g + a + 2) + S2_FREE)
                for h in range(REP):
                    one, two = (PROB[:, REP * (t % RING) + h, j:BANK] for t in (a, a + 1))
                    last = nc.gpsimd.tensor_tensor(one, one, two, ALU.add)
                last.then_inc(added, 1)
            pool.sem_inc(ctx_lo_done, CN_FREE)
            take_values(0)
            def body(g, first_group):
                cuts = {}
                for b in range(NB - 1):
                    last = TPB * (b + 1) * (b + 2) // 2 - 1
                    cuts[min(a for a in pairs if a >= last + 5)] = (g, b)
                for n, a in enumerate(pairs):
                    if a in cuts:
                        cut_context(*cuts[a])
                    add_pair(g, n)
                    if n == 0 and not first_group:
                        cut_context(g - 1, NB - 1)
                pool.wait_ge(pv_done, STEPS * g + STEPS)
                take_values((g + 1) % GROUPS)
            body(0, True)
            with pool.Fori(1, GROUPS) as g:
                body(g, False)
            cut_context(GROUPS - 1, NB - 1)


def project_context(nc, c_hi, c_lo, wo, bo, x, x1_dram, ident, x2_hi, x2_lo, sem):
    KC, T = c_hi.shape[1], c_hi.shape[2]
    D = KC * P
    PAIRS = T // P // 2
    wo_loaded, bo_loaded = [sem(f"d_wo_loaded{s}") for s in range(2)], sem("d_bo_loaded")
    wo_cut_hi, wo_cut_lo = sem("d_wo_cut_hi"), sem("d_wo_cut_lo")
    x_loaded, x1_stored = [sem(f"d_x_loaded{s}") for s in range(2)], [sem(f"d_x1_stored{s}") for s in range(2)]
    y_product, y_read, y_normed, x1_done = sem("d_y_product"), sem("d_y_read"), sem("d_y_normed"), sem("d_x1_done")
    norm_done, turned, hi_done, lo_done = sem("d_norm_done"), sem("d_turned"), sem("d_hi_done"), sem("d_lo_done")
    with ExitStack() as ctx:
        sb = lambda n, s, d=F32: ctx.enter_context(nc.sbuf_tensor("d_" + n, s, d))
        WO, BO = sb("wo", [P, 2, D]), sb("bo", [P, D])
        wo_hi, wo_lo = sb("wo_hi", [P, KC, D], F16), sb("wo_lo", [P, KC, D], F16)
        X, Y, X1, XN = (sb(n, [P, 2, D]) for n in ("x", "y", "x1", "xn"))
        y_norm = RowNorm(nc, ctx, sem, "d_y_norm", 1.0, 1.0)
        x_norm = RowNorm(nc, ctx, sem, "d_x_norm", 1.0, XS)
        YP = ctx.enter_context(nc.psum_tensor("d_yp", [P, 2, D], F32))
        XT = ctx.enter_context(nc.psum_tensor("d_xt", [P, 2, D], F32))
        block = ctx.enter_context(nc.Block())

        def tokens(i, s):
            return bass.ds((2 * i + s) * P, P)

        @block.sync
        def _(sp):
            def load_weights(k):
                sp.dma_start(WO[:, k % 2, :], wo[k * P:(k + 1) * P, :]).then_inc(wo_loaded[k % 2], 16)

            def load_rows(i):
                for s in range(2):
                    sp.dma_start(X[:, s, :], x[tokens(i, s), :]).then_inc(x_loaded[s], 16)

            def store_rows(i):
                for s in range(2):
                    sp.wait_ge(x1_done, 2 * i + s + 1)
                    sp.dma_start(x1_dram[tokens(i, s), :], X1[:, s, :]).then_inc(x1_stored[s], 16)
            load_weights(0)
            load_weights(1)
            sp.dma_start(BO[:], bo.rearrange("(o n) -> o n", o=1).broadcast_to([P, D])).then_inc(bo_loaded, 16)
            load_rows(0)
            for k in range(2, KC):
                sp.wait_ge(wo_cut_lo, k - 1)
                load_weights(k)
            with sp.Fori(0, PAIRS - 1) as i:
                store_rows(i)
                load_rows(i + 1)
            store_rows(PAIRS - 1)
            for s in range(2):
                sp.wait_ge(x1_stored[s], 16 * PAIRS)

        @block.tensor
        def _(pe):
            def product(i, first=False):
                for s in range(2):
                    if not first:
                        pe.wait_ge(y_read, 2 * i + s - 1)
                    for k in range(KC):
                        if first and s == 0:
                            pe.wait_ge(wo_cut_lo, k + 1)
                        ch, cl = (c[:, k, tokens(i, s)] for c in (c_hi, c_lo))
                        for stat, w, a, z in ((ch, wo_hi, 1, 0), (ch, wo_lo, 0, 0), (cl, wo_hi, 0, 1)):
                            for n in range(0, D, BANK):
                                last = nc.tensor.matmul(YP[:, s, n:n + BANK], stat, w[:, k, n:n + BANK],
                                                        start=(k == 0 and a == 1), stop=(k == KC - 1 and z == 1))
                    last.then_inc(y_product, 1)

            def turn(i):
                for s in range(2):
                    pe.wait_ge(norm_done, 2 * i + s + 1)
                    for c in range(KC):
                        last = nc.tensor.transpose(XT[:, s, c * P:(c + 1) * P], XN[:, s, c * P:(c + 1) * P],
                                                   ident[:])
                    last.then_inc(turned, 1)
            product(0, True)
            with pe.Fori(0, PAIRS - 1) as i:
                product(i + 1)
                turn(i)
            turn(PAIRS - 1)

        @block.vector
        def _(dve):
            for k in range(KC):
                dve.wait_ge(wo_cut_hi, k + 1)
                nc.vector.scalar_tensor_tensor(wo_lo[:, k, :], WO[:, k % 2, :], WS, wo_hi[:, k, :],
                                               ALU.mult, ALU.subtract).then_inc(wo_cut_lo, 1)
            dve.wait_ge(bo_loaded, 16)
            with dve.Fori(0, PAIRS) as i:
                for s in range(2):
                    dve.wait_ge(y_product, 2 * i + s + 1)
                    nc.vector.scalar_tensor_tensor(Y[:, s, :], YP[:, s, :], 1.0 / (CS * WS), BO[:],
                                                   ALU.mult, ALU.add).then_inc(y_read, 1)
                y_norm.on_vector(dve, i, lambda s: dve.wait_ge(y_read, 2 * i + s + 1),
                                 lambda s: Y[:, s, :], lambda s: Y[:, s, :], y_normed)
                x_norm.on_vector(dve, i, lambda s: dve.wait_ge(x1_done, 2 * i + s + 1),
                                 lambda s: X1[:, s, :], lambda s: XN[:, s, :], norm_done)
                for s in range(2):
                    dve.wait_ge(hi_done, 2 * i + s + 1)
                    nc.vector.tensor_tensor(x2_lo[:, :, tokens(i, s)], XT[:, s, :].rearrange("p (c t) -> p c t", t=P),
                                            x2_hi[:, :, tokens(i, s)], ALU.subtract).then_inc(lo_done, 1)

        @block.scalar
        def _(act):
            for k in range(KC):
                act.wait_ge(wo_loaded[k % 2], 16 * (k // 2) + 16)
                nc.scalar.activation(wo_hi[:, k, :], WO[:, k % 2, :], ACT.Copy, scale=WS).then_inc(wo_cut_hi, 1)
            with act.Fori(0, PAIRS) as i:
                y_norm.on_scalar(act, i)
                x_norm.on_scalar(act, i)
                for s in range(2):
                    act.wait_ge(turned, 2 * i + s + 1)
                    nc.scalar.activation(x2_hi[:, :, tokens(i, s)], XT[:, s, :].rearrange("p (c t) -> p c t", t=P),
                                         ACT.Copy).then_inc(hi_done, 1)

        @block.gpsimd
        def _(pool):
            def residual(i, first):
                for s in range(2):
                    if not first:
                        pool.wait_ge(x1_stored[s], 16 * i)
                    pool.wait_ge(x_loaded[s], 16 * i + 16)
                    pool.wait_ge(y_normed, 2 * i + s + 1)
                    nc.gpsimd.tensor_tensor(X1[:, s, :], X[:, s, :], Y[:, s, :], ALU.add).then_inc(x1_done, 1)
            residual(0, True)
            with pool.Fori(1, PAIRS) as i:
                residual(i, False)


def gate_and_up(nc, x2_hi, x2_lo, quantised, ident, wd_hi, wd_lo, h_hi, h_lo, sem):
    KC, T = x2_hi.shape[1], x2_hi.shape[2]
    D = KC * P
    NB = T // BANK
    (gate_q, gate_s, gate_z), (up_q, up_s, up_z), (down_q, down_s, down_z) = quantised
    inter = gate_q.shape[0]
    FULL, REST = inter // P, inter % P
    CHUNKS = FULL + (REST > 0)
    assert CHUNKS % 2 == 0 and 0 < REST and REST % QGROUP == 0 and NB == 4
    GROUPS_IN, GROUPS_MID = D // QGROUP, inter // QGROUP
    GATE, UP, DOWN = range(3)
    in_scale = 1.0 / (XS * WS)

    tables_loaded, raw_loaded = sem("e_tables_loaded"), [sem(f"e_raw_loaded{s}") for s in range(2)]
    unpacked, shifted, scaled = sem("e_unpacked"), sem("e_shifted"), sem("e_scaled")
    turned, cut_hi, cut_lo = sem("e_turned"), sem("e_cut_hi"), sem("e_cut_lo")
    gate_product, up_product, silu_done = sem("e_gate_product"), sem("e_up_product"), sem("e_silu_done")
    h_done, hi_done, lo_done, cleared = (sem(f"e_{n}") for n in ("h_done", "hi_done", "lo_done", "cleared"))
    hi_stored, lo_stored = ([sem(f"e_{n}_stored{s}") for s in range(2)] for n in ("hi", "lo"))
    FREE = 2

    with ExitStack() as ctx:
        sb = lambda n, s, d=F32: ctx.enter_context(nc.sbuf_tensor("e_" + n, s, d))
        scales = [sb(f"{n}_s", [P, CHUNKS, GROUPS_IN]) for n in ("gate", "up")] + [sb("down_s", [P, KC, GROUPS_MID])]
        zeros = [sb(f"{n}_z", [P, CHUNKS, GROUPS_IN]) for n in ("gate", "up")] + [sb("down_z", [P, KC, GROUPS_MID])]
        RAW, NIBBLES = sb("raw", [P, 2, D // 2], I32), sb("nibbles", [P, D], I32)
        W = sb("w", [P, 2, D])
        w_hi, w_lo = (sb(n, [P, 2, 2, KC, P], F16) for n in ("w_hi", "w_lo"))
        SILU, H = sb("silu", [P, 2, BANK]), sb("h", [P, 2, BANK])
        HH, HL = sb("hh", [P, 2, BANK], F16), sb("hl", [P, 2, BANK], F16)
        WT = ctx.enter_context(nc.psum_tensor("e_wt", [P, 2, D], F32))
        GP = ctx.enter_context(nc.psum_tensor("e_gp", [P, 2, BANK], F32))
        UP_ = ctx.enter_context(nc.psum_tensor("e_up", [P, 2, BANK], F32))
        block = ctx.enter_context(nc.Block())

        def number(chunk):
            return 2 * chunk[0] + chunk[1]

        def height(chunk):
            c = number(chunk)
            return REST if isinstance(c, int) and c == FULL else P

        def after(chunk):
            j, parity = chunk
            return (j, 1) if parity == 0 else (j + 1, 0)

        def weights(chunk, kind):
            j, parity = chunk
            return 6 * j + 3 * parity + kind, (parity + kind) % 2

        def wait_positive(eng, signal, value):
            if not (isinstance(value, int) and value <= 0):
                eng.wait_ge(signal, value)

        def extent(kind, chunk):
            n = height(chunk)
            return (P, KC * n // 2) if kind == DOWN else (n, D // 2)

        def table(t, kind, chunk):
            n = height(chunk)
            if kind != DOWN:
                return t[kind][0:n, number(chunk), :].unsqueeze(2).broadcast_to([n, GROUPS_IN, QGROUP])
            at = bass.ds(number(chunk) * (P // QGROUP), n // QGROUP)
            return t[kind][:, :, at].unsqueeze(3).broadcast_to([P, KC, n // QGROUP, QGROUP])

        def grouped(ap, kind, chunk):
            rows, packed = extent(kind, chunk)
            flat = ap[0:rows, 0:2 * packed]
            if kind != DOWN:
                return flat.rearrange("p (g j) -> p g j", j=QGROUP)
            return flat.rearrange("p (k g j) -> p k g j", k=KC, j=QGROUP)

        def turned_parts(kind, chunk):
            n, (_, slot) = height(chunk), weights(chunk, kind)
            if kind == DOWN:
                return WT[0:n, slot, :], wd_hi[0:n, number(chunk), :], wd_lo[0:n, number(chunk), :]
            at = (slice(None), kind, chunk[1], slice(None), slice(0, n))
            return WT[:, slot, :].rearrange("p (k i) -> p k i", i=P)[:, :, 0:n], w_hi[at], w_lo[at]

        def all_chunks(eng, prepare, multiply):
            for kind in range(3):
                prepare((0, 0), kind)
            with eng.Fori(0, FULL // 2) as j:
                for parity in range(2):
                    multiply((j, parity), after((j, parity)))
            multiply((FULL // 2, 0), (FULL // 2, 1))
            multiply((FULL // 2, 1), None)

        @block.sync
        def _(sp):
            for t, (_, s_, z_) in enumerate(quantised[:2]):
                for buf, src in ((scales[t], s_), (zeros[t], z_)):
                    sp.dma_start(buf[:, 0:FULL, :], src[0:FULL * P, :].rearrange("(c p) g -> p c g", p=P)
                                 ).then_inc(tables_loaded, 16)
                    sp.dma_start(buf[0:REST, FULL, :], src[FULL * P:, :]).then_inc(tables_loaded, 16)
            for buf, src in ((scales[DOWN], down_s), (zeros[DOWN], down_z)):
                sp.dma_start(buf[:], src.rearrange("(k p) g -> p k g", p=P)).then_inc(tables_loaded, 16)
            for s in range(2):
                sp.sem_inc(hi_stored[s], 16)
                sp.sem_inc(lo_stored[s], 16)

            def prepare(chunk, kind):
                m, slot = weights(chunk, kind)
                n, c = height(chunk), number(chunk)
                rows, packed = extent(kind, chunk)
                wait_positive(sp, unpacked, m - 1)
                if kind == DOWN:
                    dst = RAW[:, slot, 0:packed].rearrange("p (k i) -> p k i", k=KC)
                    src = down_q[:, bass.ds(c * (P // 2), n // 2)].rearrange("(k p) i -> p k i", p=P)
                else:
                    dst, src = RAW[0:n, slot, :], (gate_q, up_q)[kind][bass.ds(c * P, n), :]
                sp.dma_start(dst, src).then_inc(raw_loaded[slot], 16)

            def multiply(chunk, coming):
                c, n = number(chunk), height(chunk)
                for b in range(NB):
                    if coming and b < 3:
                        prepare(coming, b)
                    for buf, done, dram, stored in ((HH, hi_done, h_hi, hi_stored), (HL, lo_done, h_lo, lo_stored)):
                        sp.wait_ge(done, NB * c + b + 1 + (FREE if done is lo_done else 0))
                        sp.dma_start(dram[bass.ds(c * P, n), b * BANK:(b + 1) * BANK], buf[0:n, b % 2, :]
                                     ).then_inc(stored[b % 2], 16)
            all_chunks(sp, prepare, multiply)
            for s in range(2):
                sp.wait_ge(hi_stored[s], 16 * (NB // 2 * CHUNKS + 1))
                sp.wait_ge(lo_stored[s], 16 * (NB // 2 * CHUNKS + 1))

        @block.tensor
        def _(pe):
            def prepare(chunk, kind):
                m, slot = weights(chunk, kind)
                n = height(chunk)
                wait_positive(pe, cut_lo, m - 1)
                pe.wait_ge(scaled, m + 1)
                for k in range(KC):
                    if kind == DOWN:
                        last = nc.tensor.transpose(WT[0:n, slot, k * P:(k + 1) * P], W[:, slot, k * n:(k + 1) * n],
                                                   ident[:])
                    else:
                        last = nc.tensor.transpose(WT[:, slot, k * P:k * P + n], W[0:n, slot, k * P:(k + 1) * P],
                                                   ident[0:n, 0:n])
                last.then_inc(turned, 1)

            def multiply(chunk, coming):
                c, n, parity = number(chunk), height(chunk), chunk[1]
                for b in range(NB):
                    if b == 0:
                        pe.wait_ge(cut_lo, 6 * chunk[0] + 3 * parity + 2)
                    pe.wait_ge(h_done, NB * c + b - 1 + FREE)
                    tok = slice(b * BANK, (b + 1) * BANK)
                    for kind, out, done in ((GATE, GP, gate_product), (UP, UP_, up_product)):
                        o = out[0:n, b % 2, :]
                        for k in range(KC):
                            wh, wl = (w[:, kind, parity, k, 0:n] for w in (w_hi, w_lo))
                            nc.tensor.matmul(o, wh, x2_hi[:, k, tok], start=(k == 0), stop=False)
                            nc.tensor.matmul(o, wh, x2_lo[:, k, tok], start=False, stop=False)
                            last = nc.tensor.matmul(o, wl, x2_hi[:, k, tok], start=False, stop=(k == KC - 1))
                        last.then_inc(done, 1)
                    if coming and b < 3:
                        prepare(coming, b)
            all_chunks(pe, prepare, multiply)

        @block.vector
        def _(dve):
            dve.sem_inc(h_done, FREE)
            dve.wait_ge(tables_loaded, 16 * 10)

            def unpack(chunk, kind):
                m, slot = weights(chunk, kind)
                rows, packed = extent(kind, chunk)
                wait_positive(dve, shifted, m)
                dve.wait_ge(raw_loaded[slot], 16 * (3 * chunk[0] + (3 * chunk[1] + kind) // 2 + 1))
                raw = RAW[0:rows, slot, 0:packed]
                pair = NIBBLES[0:rows, 0:2 * packed].rearrange("p (j two) -> p two j", two=2)
                nc.vector.tensor_scalar(pair[:, 0, :], raw, 4, 15, ALU.logical_shift_right, ALU.bitwise_and)
                nc.vector.tensor_scalar(pair[:, 1, :], raw, 15, None, ALU.bitwise_and).then_inc(unpacked, 1)
                wait_positive(dve, turned, m - 1)
                dve.wait_ge(unpacked, m + 1)
                nc.vector.tensor_tensor(grouped(W[:, slot], kind, chunk), grouped(NIBBLES, kind, chunk),
                                        table(zeros, kind, chunk), ALU.subtract).then_inc(shifted, 1)

            def cut(chunk, kind):
                m, _ = weights(chunk, kind)
                psum, hi, lo = turned_parts(kind, chunk)
                dve.wait_ge(cut_hi, m + 1)
                nc.vector.scalar_tensor_tensor(lo, psum, WS, hi, ALU.mult, ALU.subtract).then_inc(cut_lo, 1)

            def prepare(chunk, kind):
                unpack(chunk, kind)
                cut(chunk, kind)

            def multiply(chunk, coming):
                c, n = number(chunk), height(chunk)
                for b in range(NB):
                    if coming and b < 3:
                        unpack(coming, b)
                    dve.wait_ge(lo_done, NB * c + b - 1 + FREE)
                    dve.wait_ge(silu_done, NB * c + b + 1)
                    dve.wait_ge(up_product, NB * c + b + 1)
                    nc.vector.scalar_tensor_tensor(H[0:n, b % 2, :], UP_[0:n, b % 2, :], HS * in_scale,
                                                   SILU[0:n, b % 2, :], ALU.mult, ALU.mult).then_inc(h_done, 1)
                    if coming and b < 3:
                        cut(coming, b)
            all_chunks(dve, prepare, multiply)

        @block.scalar
        def _(act):
            def prepare(chunk, kind):
                m, _ = weights(chunk, kind)
                psum, hi, lo = turned_parts(kind, chunk)
                act.wait_ge(turned, m + 1)
                nc.scalar.activation(hi, psum, ACT.Copy, scale=WS).then_inc(cut_hi, 1)

            def multiply(chunk, coming):
                c, n = number(chunk), height(chunk)
                for b in range(NB):
                    act.wait_ge(gate_product, NB * c + b + 1)
                    nc.scalar.activation(SILU[0:n, b % 2, :], GP[0:n, b % 2, :], ACT.Silu, scale=in_scale
                                         ).then_inc(silu_done, 1)
                    act.wait_ge(hi_stored[b % 2], 16 * (NB // 2 * c + b // 2 + 1))
                    act.wait_ge(lo_done, NB * c + b - 1 + FREE)
                    act.wait_ge(h_done, NB * c + b + 1 + FREE)
                    nc.scalar.activation(HH[0:n, b % 2, :], H[0:n, b % 2, :], ACT.Copy).then_inc(hi_done, 1)
                    if coming and b < 3:
                        prepare(coming, b)
            all_chunks(act, prepare, multiply)

        @block.gpsimd
        def _(pool):
            pool.sem_inc(lo_done, FREE)
            for w in (wd_hi, wd_lo):
                last = nc.gpsimd.memset(w[REST:P, FULL, :], 0.0)
            last.then_inc(cleared, 1)
            pool.wait_ge(cleared, 1)
            pool.wait_ge(tables_loaded, 16 * 10)

            def prepare(chunk, kind):
                m, slot = weights(chunk, kind)
                pool.wait_ge(shifted, m + 1)
                nc.gpsimd.tensor_tensor(grouped(W[:, slot], kind, chunk), grouped(W[:, slot], kind, chunk),
                                        table(scales, kind, chunk), ALU.mult).then_inc(scaled, 1)

            def multiply(chunk, coming):
                c, n = number(chunk), height(chunk)
                for b in range(NB):
                    if coming and b < 3:
                        prepare(coming, b)
                    pool.wait_ge(lo_stored[b % 2], 16 * (NB // 2 * c + b // 2 + 1))
                    pool.wait_ge(hi_done, NB * c + b + 1)
                    nc.gpsimd.tensor_tensor(HL[0:n, b % 2, :], H[0:n, b % 2, :], HH[0:n, b % 2, :], ALU.subtract
                                            ).then_inc(lo_done, 1)
            all_chunks(pool, prepare, multiply)


def project_down(nc, h_hi, h_lo, wd_hi, wd_lo, x1_dram, out, sem):
    CHUNKS, D = wd_hi.shape[1], wd_hi.shape[2]
    inter, T = h_hi.shape
    FULL, REST = inter // P, inter % P
    BLOCK = 2 * P
    ROUNDS = T // BLOCK // 2
    h_loaded = [sem(f"f_h_loaded{u}") for u in range(2)]
    x_loaded = [sem(f"f_x_loaded{u}") for u in range(2)]
    stored = [sem(f"f_stored{u}") for u in range(2)]
    product, normed, added, cleared = sem("f_product"), sem("f_normed"), sem("f_added"), sem("f_cleared")
    with ExitStack() as ctx:
        sb = lambda n, s, d=F32: ctx.enter_context(nc.sbuf_tensor("f_" + n, s, d))
        H_HI, H_LO = (sb(n, [P, 2, CHUNKS, BLOCK], F16) for n in ("h_hi", "h_lo"))
        X = sb("x", [P, 2, 2, D])
        Z = sb("z", [P, 2, 2, D])
        norm = RowNorm(nc, ctx, sem, "f_norm", HS * WS, 1.0)
        YP = ctx.enter_context(nc.psum_tensor("f_yp", [P, 2, 2, D], F32))
        block = ctx.enter_context(nc.Block())

        def rows(i, u):
            return bass.ds((2 * i + u) * BLOCK, BLOCK)

        @block.sync
        def _(sp):
            def load(i, u):
                for buf, src in ((H_HI, h_hi), (H_LO, h_lo)):
                    sp.dma_start(buf[:, u, 0:FULL, :], src[0:FULL * P, rows(i, u)].rearrange("(c p) t -> p c t", p=P)
                                 ).then_inc(h_loaded[u], 16)
                    sp.dma_start(buf[0:REST, u, FULL, :], src[FULL * P:, rows(i, u)]).then_inc(h_loaded[u], 16)
                sp.dma_start(X[:, u], x1_dram[rows(i, u), :].rearrange("(s p) d -> p s d", p=P)
                             ).then_inc(x_loaded[u], 16)

            def store(i, u):
                sp.wait_ge(added, 4 * i + 2 * u + 2)
                sp.dma_start(out[rows(i, u), :].rearrange("(s p) d -> p s d", p=P), Z[:, u]).then_inc(stored[u], 16)
            load(0, 0)
            load(0, 1)
            with sp.Fori(0, ROUNDS - 1) as i:
                for u in range(2):
                    store(i, u)
                    load(i + 1, u)
            for u in range(2):
                store(ROUNDS - 1, u)
            for u in range(2):
                sp.wait_ge(stored[u], 16 * ROUNDS)

        @block.tensor
        def _(pe):
            pe.wait_ge(cleared, 1)

            def block_product(i, u, first):
                pe.wait_ge(h_loaded[u], 64 * i + 64)
                for s in range(2):
                    if not first:
                        pe.wait_ge(normed, 4 * i + 2 * u + s - 3)
                    for c in range(CHUNKS):
                        hh, hl = (h[:, u, c, s * P:(s + 1) * P] for h in (H_HI, H_LO))
                        for stat, w, a, z in ((hh, wd_hi, 1, 0), (hh, wd_lo, 0, 0), (hl, wd_hi, 0, 1)):
                            for n in range(0, D, BANK):
                                last = nc.tensor.matmul(YP[:, u, s, n:n + BANK], stat, w[:, c, n:n + BANK],
                                                        start=(c == 0 and a == 1), stop=(c == CHUNKS - 1 and z == 1))
                    last.then_inc(product, 1)
            block_product(0, 0, True)
            block_product(0, 1, True)
            with pe.Fori(1, ROUNDS) as i:
                for u in range(2):
                    block_product(i, u, False)

        @block.vector
        def _(dve):
            def normalise(i, u, first):
                if not first:
                    dve.wait_ge(stored[u], 16 * i)
                norm.on_vector(dve, 2 * i + u, lambda s: dve.wait_ge(product, 4 * i + 2 * u + s + 1),
                               lambda s: YP[:, u, s, :], lambda s: Z[:, u, s, :], normed)
            normalise(0, 0, True)
            normalise(0, 1, True)
            with dve.Fori(1, ROUNDS) as i:
                for u in range(2):
                    normalise(i, u, False)

        @block.scalar
        def _(act):
            with act.Fori(0, 2 * ROUNDS) as r:
                norm.on_scalar(act, r)

        @block.gpsimd
        def _(pool):
            for h in (H_HI, H_LO):
                last = nc.gpsimd.memset(h[REST:P, :, FULL, :], 0.0)
            last.then_inc(cleared, 1)
            pool.wait_ge(cleared, 1)
            with pool.Fori(0, ROUNDS) as i:
                for u in range(2):
                    pool.wait_ge(x_loaded[u], 16 * i + 16)
                    for s in range(2):
                        pool.wait_ge(normed, 4 * i + 2 * u + s + 1)
                        nc.gpsimd.tensor_tensor(Z[:, u, s, :], X[:, u, s, :], Z[:, u, s, :], ALU.add
                                                ).then_inc(added, 1)


def sandwich_layer(nc, x, wq, wkv, wo, bo, gate_q, up_q, down_q, gate_s, gate_z, up_s, up_z,
                   down_s, down_z, out, debug=None):
    T, D = x.shape
    NT, KC = T // P, D // P
    VC = wkv.shape[1] // 2
    QK = D + VC
    inter = gate_q.shape[0]
    qk_hi, qk_lo = (nc.dram_tensor(n, (QK, T), F16).ap() for n in ("qk_hi", "qk_lo"))
    h_hi, h_lo = (nc.dram_tensor(n, (inter, T), F16).ap() for n in ("h_hi", "h_lo"))
    x1_dram = nc.dram_tensor("x1_dram", (T, D), F32).ap()
    with ExitStack() as whole:
        def sem(name):
            return whole.enter_context(nc.semaphore(name))

        def tensor(stack, name, shape, dtype, side="left"):
            return stack.enter_context(nc.sbuf_tensor(name, shape, dtype, side=side))
        ident, identb = tensor(whole, "ident", [P, P], F32), tensor(whole, "identb", [P, P], BF16)
        causal, ones = tensor(whole, "causal", [P, P], BF16), tensor(whole, "ones", [P, D // HEADS], F32)
        build_constants(nc, ident, identb, causal, ones, sem)
        with ExitStack() as context:
            c_hi, c_lo = (tensor(context, n, [P, KC, T], F16) for n in ("c_hi", "c_lo"))
            with ExitStack() as attention:
                v_sb = tensor(attention, "v_sb", [P, NT, VC], F32, "right")
                with ExitStack() as stage:
                    w_hi, w_lo = (tensor(stage, n, [P, KC, QK + VC], F16) for n in ("w_hi", "w_lo"))
                    project_qkv(nc, x, wq, wkv, ident, c_hi, c_lo, w_hi, w_lo, qk_hi, qk_lo, v_sb, sem)
                if debug == "qkv":
                    return
                attend(nc, qk_hi, qk_lo, v_sb, ident, identb, causal, ones, c_hi, c_lo, sem)
            if debug == "attn":
                dbg = nc.dram_tensor("ctx_dbg", (D, T), F32).ap()
                n = sem("dbg")
                with nc.Block() as block:
                    @block.gpsimd
                    def _(e):
                        e.dma_start(dbg.rearrange("(c p) t -> p c t", p=P), c_hi[:]).then_inc(n, 16)
                        e.wait_ge(n, 16)
                return
            ffn = whole.enter_context(ExitStack())
            x2_hi, x2_lo = (tensor(ffn, n, [P, KC, T], F16, "right") for n in ("x2_hi", "x2_lo"))
            project_context(nc, c_hi, c_lo, wo, bo, x, x1_dram, ident, x2_hi, x2_lo, sem)
        if debug == "x1":
            return
        wd_hi, wd_lo = (tensor(whole, n, [P, -(-inter // P), D], F16) for n in ("wd_hi", "wd_lo"))
        gate_and_up(nc, x2_hi, x2_lo, ((gate_q, gate_s, gate_z), (up_q, up_s, up_z), (down_q, down_s, down_z)),
                    ident, wd_hi, wd_lo, h_hi, h_lo, sem)
        ffn.close()
        project_down(nc, h_hi, h_lo, wd_hi, wd_lo, x1_dram, out, sem)


INPUTS = ["L0_attn_x", "L0_attn_Wq", "L0_attn_Wkv", "L0_attn_Wo", "L0_attn_bo", "L0_ffn_gate_Wq", "L0_ffn_up_Wq",
          "L0_ffn_down_Wq", "L0_ffn_gate_scale", "L0_ffn_gate_zero", "L0_ffn_up_scale", "L0_ffn_up_zero",
          "L0_ffn_down_scale", "L0_ffn_down_zero"]


def kernel(**inputs):
    import numpy as np
    from concourse import bacc
    from concourse.bass_utils import run_bass_kernel_spmd

    nc = bacc.Bacc("TRN2", target_bir_lowering=False, num_devices=1)
    arrays, args = {}, []
    shape = np.shape(inputs["L0_attn_x"])
    for name in INPUTS:
        a = np.ascontiguousarray(inputs[name])
        if name == "L0_attn_x":
            a = a.reshape(shape[1:])
        arrays[name] = a
        args.append(nc.dram_tensor(name, a.shape, mybir.dt.from_np(a.dtype), kind="ExternalInput").ap())
    args.append(nc.dram_tensor("out", shape[1:], F32, kind="ExternalOutput").ap())
    sandwich_layer(nc, *args)
    result = run_bass_kernel_spmd(nc, [arrays], core_ids=[0])
    return result.results[0]["out"].reshape(shape)
```

```python
from contextlib import ExitStack

import concourse.bass as bass
from concourse import mybir

P = 128
BANK = 512
F32, F16, BF16, I32 = mybir.dt.float32, mybir.dt.float16, mybir.dt.bfloat16, mybir.dt.int32
ALU = mybir.AluOpType
ACT = mybir.ActivationFunctionType
AX = mybir.AxisListType

EPS = 1e-5
HEADS, GROUPS = 32, 8
QGROUP = 64
XS = 16.0
WS = 1024.0
QS = 16.0
CS = 64.0
HS = 16.0
MS = QS * QS
MASKED = -1.0e30
LEAST = -3.0e38


def build_constants(nc, ident, identb, causal, ones, sem):
    zeroed, made = sem("consts_zeroed"), sem("consts_made")
    with nc.Block() as block:
        @block.gpsimd
        def _(pool):
            nc.gpsimd.memset(ident[:], 0.0)
            nc.gpsimd.memset(identb[:], 0.0)
            nc.gpsimd.memset(ones[:], 1.0)
            nc.gpsimd.memset(causal[:], 0.0).then_inc(zeroed, 1)
            pool.wait_ge(zeroed, 1)
            for m in (ident, identb):
                nc.gpsimd.affine_select(out=m[:], in_=m[:], compare_op=ALU.not_equal, fill=1.0, base=0,
                                        pattern=[[-1, P]], channel_multiplier=1)
            nc.gpsimd.affine_select(out=causal[:], in_=causal[:], compare_op=ALU.is_ge, fill=MASKED, base=0,
                                    pattern=[[-1, P]], channel_multiplier=1).then_inc(made, 1)


class RowNorm:

    def __init__(self, nc, ctx, sem, name, in_scale, out_scale):
        self.nc = nc
        self.keep, self.root_scale = in_scale ** -2, (in_scale / out_scale) ** 2
        sb = lambda n, s: ctx.enter_context(nc.sbuf_tensor(f"{name}_{n}", s, F32))
        self.stats, self.mv = sb("stats", [P, 2, 2, 6]), sb("mv", [P, 2, 2])
        self.var, self.root, self.rstd = sb("var", [P, 2]), sb("root", [P, 2]), sb("rstd", [P, 2])
        self.stats_done, self.stats_seen, self.aggr_done, self.var_done, self.root_done, self.rstd_done = (
            sem(f"{name}_{n}") for n in
            ("stats_done", "stats_seen", "aggr_done", "var_done", "root_done", "rstd_done"))

    def on_vector(self, dve, r, wait_source, source, target, done):
        nc = self.nc
        for s in range(2):
            wait_source(s)
            rows = source(s)
            half = rows.shape[-1] // 2
            nc.vector.bn_stats(self.stats[:, s, 0, :], rows[:, 0:half])
            nc.vector.bn_stats(self.stats[:, s, 1, :], rows[:, half:]).then_inc(self.stats_done, 1)
        dve.wait_ge(self.stats_done, 2 * r + 2)
        dve.sem_inc(self.stats_seen, 1)
        for s in range(2):
            nc.vector.bn_aggr(self.mv[:, s, :], self.stats[:, s, :, :]).then_inc(self.aggr_done, 1)
        dve.wait_ge(self.aggr_done, 2 * r + 2)
        nc.vector.tensor_scalar(self.var[:], self.mv[:, :, 1], self.keep, EPS, ALU.mult, ALU.add
                                ).then_inc(self.var_done, 1)
        dve.wait_ge(self.root_done, r + 1)
        nc.vector.reciprocal(self.rstd[:], self.root[:]).then_inc(self.rstd_done, 1)
        dve.wait_ge(self.rstd_done, r + 1)
        for s in range(2):
            nc.vector.tensor_scalar(target(s), source(s), self.mv[:, s, 0:1], self.rstd[:, s:s + 1],
                                    ALU.subtract, ALU.mult).then_inc(done, 1)

    def on_scalar(self, act, r):
        act.wait_ge(self.var_done, r + 1)
        self.nc.scalar.activation(self.root[:], self.var[:], ACT.Sqrt, scale=self.root_scale
                                  ).then_inc(self.root_done, 1)


def project_qk(nc, x, wq, wkv, ident, x_hi, x_lo, w_hi, w_lo, wv_hi, wv_lo, qk_hi, qk_lo, sem):
    T, D = x.shape
    KC = D // P
    QK = qk_hi.shape[0]
    NB, TILES, COLS = T // BANK, BANK // P, QK // P
    VC = wv_hi.shape[2]
    RING = 5
    WBUF = 4
    assert COLS == 2 * RING
    TURN_AFTER = {2: 0, 4: 1, 7: 2, 8: 3}
    NORM_AFTER = {0: 0, 4: 1}
    x_loaded = [sem(f"b_x_loaded{s}") for s in range(TILES)]
    w_loaded = [sem(f"b_w_loaded{s}") for s in range(WBUF)]
    w_cut_hi, w_cut_lo = sem("b_w_cut_hi"), sem("b_w_cut_lo")
    norm_done, turned, x_cut_hi, x_cut_lo = (sem("b_" + n) for n in ("norm_done", "turned", "x_cut_hi", "x_cut_lo"))
    product, hi_done, lo_done = sem("b_product"), sem("b_hi_done"), sem("b_lo_done")
    hi_stored = [sem(f"b_hi_stored{b}") for b in range(RING)]
    lo_stored = [sem(f"b_lo_stored{b}") for b in range(RING)]
    out_scale = QS / (XS * WS)
    with ExitStack() as ctx:
        sb = lambda n, s, d=F32: ctx.enter_context(nc.sbuf_tensor("b_" + n, s, d))
        X, XN = sb("x", [P, TILES, D]), sb("xn", [P, TILES, D])
        W = sb("w", [P, WBUF, D + 2 * VC])
        HI, LO = sb("hi", [P, RING, BANK], F16), sb("lo", [P, RING, BANK], F16)
        norm = RowNorm(nc, ctx, sem, "b_norm", 1.0, XS)
        XT = ctx.enter_context(nc.psum_tensor("b_xt", [P, KC * P], F32))
        PS = ctx.enter_context(nc.psum_tensor("b_ps", [P, RING, BANK], F32))
        block = ctx.enter_context(nc.Block())

        def turned_rows(b, s):
            if isinstance(b, int) and b == 0 and s in (1, 2):
                return PS[:, 2 * s - 2:2 * s, :].rearrange("p c t -> p (c t)")
            return XT[:]

        def of_kind(ap, kind):
            return ap.rearrange("p (g two d) -> p two g d", two=2, g=GROUPS)[:, kind]

        def columns(w, wv, i, kind):
            return (wv[:, i, :] if kind else w[:, i, D:D + VC]).rearrange("p (g d) -> p g d", g=GROUPS)

        def tile(x, b, s):
            return x[:, :, bass.ds((TILES * b + s) * P, P)]

        def all_blocks(eng, body):
            body(0, first=True, last=False)
            with eng.Fori(1, NB - 1) as b:
                body(b, first=False, last=False)
            body(NB - 1, first=False, last=True)

        @block.sync
        def _(sp):
            def load_tile(b, s):
                sp.dma_start(X[:, s, :], x[bass.ds((TILES * b + s) * P, P), :]).then_inc(x_loaded[s], 16)

            def body(b, first, last):
                if not last:
                    for s in range(TILES):
                        sp.wait_ge(norm_done, TILES * b + s + 1)
                        load_tile(b + 1, s)
                for c in range(COLS):
                    r = c % RING
                    sp.wait_ge(hi_done, COLS * b + c + 1)
                    sp.dma_start(qk_hi[c * P:(c + 1) * P, bass.ds(b * BANK, BANK)], HI[:, r, :]
                                 ).then_inc(hi_stored[r], 16)
                    sp.wait_ge(lo_done, COLS * b + c + 1)
                    sp.dma_start(qk_lo[c * P:(c + 1) * P, bass.ds(b * BANK, BANK)], LO[:, r, :]
                                 ).then_inc(lo_stored[r], 16)
            for s in range(TILES):
                load_tile(0, s)
            for i in range(KC):
                if i >= WBUF:
                    sp.wait_ge(w_cut_lo, 3 * (i - WBUF) + 3)
                sp.dma_start(W[:, i % WBUF, 0:D], wq[i * P:(i + 1) * P, :]).then_inc(w_loaded[i % WBUF], 16)
                sp.dma_start(W[:, i % WBUF, D:], wkv[i * P:(i + 1) * P, :]).then_inc(w_loaded[i % WBUF], 16)
            all_blocks(sp, body)
            for r in range(RING):
                sp.wait_ge(hi_stored[r], 16 * 2 * NB)
                sp.wait_ge(lo_stored[r], 16 * 2 * NB)

        @block.tensor
        def _(pe):
            def turn(b, s):
                pe.wait_ge(norm_done, TILES * b + s + 1)
                if isinstance(b, int) and b == 0:
                    if s == 3:
                        pe.wait_ge(x_cut_lo, 1)
                else:
                    pe.wait_ge(x_cut_lo, TILES * b + s)
                for c in range(KC):
                    last = nc.tensor.transpose(turned_rows(b, s)[:, c * P:(c + 1) * P], XN[:, s, c * P:(c + 1) * P], ident[:])
                last.then_inc(turned, 1)

            def column_chunk(b, c, k):
                wh, wl = (w[:, k, c * P:(c + 1) * P] for w in (w_hi, w_lo))
                xh, xl = (x[:, k, bass.ds(b * BANK, BANK)] for x in (x_hi, x_lo))
                o = PS[:, c % RING, :]
                nc.tensor.matmul(o, wh, xh, start=(k == 0), stop=False)
                nc.tensor.matmul(o, wh, xl, start=False, stop=False)
                return nc.tensor.matmul(o, wl, xh, start=False, stop=(k == KC - 1))

            def body(b, first, last):
                pe.wait_ge(x_cut_lo, TILES * b + TILES)
                if first:
                    for k in range(KC):
                        pe.wait_ge(w_cut_lo, 3 * k + 3)
                        for c in range(RING):
                            done = column_chunk(b, c, k)
                            if k == KC - 1:
                                done.then_inc(product, 1)
                for c in range(COLS):
                    if not (first and c < RING):
                        pe.wait_ge(lo_done, COLS * b + c + 1 - RING)
                        for k in range(KC):
                            done = column_chunk(b, c, k)
                        done.then_inc(product, 1)
                    if c in TURN_AFTER and not last:
                        turn(b + 1, TURN_AFTER[c])
            for s in range(TILES):
                turn(0, s)
            all_blocks(pe, body)

        @block.scalar
        def _(act):
            def cut_tile(b, s):
                act.wait_ge(turned, TILES * b + s + 1)
                nc.scalar.activation(tile(x_hi, b, s), turned_rows(b, s).rearrange("p (c t) -> p c t", t=P),
                                     ACT.Copy).then_inc(x_cut_hi, 1)

            def body(b, first, last):
                for c in range(COLS):
                    if not (first and c < RING):
                        act.wait_ge(hi_stored[c % RING], 16 * (2 * b + c // RING))
                    act.wait_ge(product, COLS * b + c + 1)
                    nc.scalar.activation(HI[:, c % RING, :], PS[:, c % RING, :], ACT.Copy, scale=out_scale
                                         ).then_inc(hi_done, 1)
                    if not last:
                        if c in NORM_AFTER:
                            norm.on_scalar(act, 2 * (b + 1) + NORM_AFTER[c])
                        if c in TURN_AFTER:
                            cut_tile(b + 1, TURN_AFTER[c])
            for pair in range(2):
                norm.on_scalar(act, pair)
            for s in range(TILES):
                cut_tile(0, s)
            for i in range(KC):
                act.wait_ge(w_loaded[i % WBUF], 32 * (i // WBUF) + 32)
                nc.scalar.activation(w_hi[:, i, 0:D], W[:, i % WBUF, 0:D], ACT.Copy, scale=WS).then_inc(w_cut_hi, 1)
                for kind in range(2):
                    nc.scalar.activation(columns(w_hi, wv_hi, i, kind), of_kind(W[:, i % WBUF, D:], kind),
                                         ACT.Copy, scale=WS).then_inc(w_cut_hi, 1)
            all_blocks(act, body)

        @block.vector
        def _(dve):
            def normalise_pair(b, pair):
                at = 2 * pair
                norm.on_vector(dve, 2 * b + pair, lambda s: dve.wait_ge(x_loaded[at + s], 16 * b + 16),
                               lambda s: X[:, at + s, :], lambda s: XN[:, at + s, :], norm_done)

            def cut_tile(b, s):
                dve.wait_ge(x_cut_hi, TILES * b + s + 1)
                nc.vector.tensor_tensor(tile(x_lo, b, s), turned_rows(b, s).rearrange("p (c t) -> p c t", t=P),
                                        tile(x_hi, b, s), ALU.subtract).then_inc(x_cut_lo, 1)

            def body(b, first, last):
                for c in range(COLS):
                    if not (first and c < RING):
                        dve.wait_ge(lo_stored[c % RING], 16 * (2 * b + c // RING))
                    dve.wait_ge(hi_done, COLS * b + c + 1)
                    nc.vector.scalar_tensor_tensor(LO[:, c % RING, :], PS[:, c % RING, :], out_scale,
                                                   HI[:, c % RING, :], ALU.mult, ALU.subtract).then_inc(lo_done, 1)
                    if not last:
                        if c in NORM_AFTER:
                            normalise_pair(b + 1, NORM_AFTER[c])
                        if c in TURN_AFTER:
                            cut_tile(b + 1, TURN_AFTER[c])
            for pair in range(2):
                normalise_pair(0, pair)
            for s in range(TILES):
                cut_tile(0, s)
            for i in range(KC):
                dve.wait_ge(w_cut_hi, 3 * i + 3)
                nc.vector.scalar_tensor_tensor(w_lo[:, i, 0:D], W[:, i % WBUF, 0:D], WS, w_hi[:, i, 0:D],
                                               ALU.mult, ALU.subtract).then_inc(w_cut_lo, 1)
                for kind in range(2):
                    nc.vector.scalar_tensor_tensor(
                        columns(w_lo, wv_lo, i, kind), of_kind(W[:, i % WBUF, D:], kind), WS, columns(w_hi, wv_hi, i, kind),
                        ALU.mult, ALU.subtract).then_inc(w_cut_lo, 1)
            all_blocks(dve, body)


def attend(nc, x_hi, x_lo, wv_hi, wv_lo, qk_hi, qk_lo, v_sb, ident, identb, causal, ones, c_hi, c_lo, sem):
    T = qk_hi.shape[1]
    D = c_hi.shape[1] * P
    HD = D // HEADS
    NT, NB, REP = T // P, T // BANK, HEADS // GROUPS
    TPB = BANK // P
    STACK = 3 * HD
    UNIT = 2 * BANK
    RING = 5
    exp_scale = float(HD) ** -0.5 / MS
    VC = wv_hi.shape[2]

    steps = [(b, k) for b in range(NB) for k in range(TPB * (b + 1))]
    STEPS = len(steps)
    last_of = {s: b for s, (b, k) in enumerate(steps) if k == TPB * (b + 1) - 1}
    assert T == 2 * UNIT
    half = NT // 2
    units = [unit for h in range(REP) for a in range(half)
             for unit in ((h, half + a, 0), (h, a, 0), (h, NT - 1 - a, 1))]
    UNITS = len(units)
    EARLY = NT // 4
    PART = UNITS // (2 * (NT - EARLY))
    SLOTS = UNITS + 1
    width = [BANK - max(0, k - TPB * b) * P for b, k in steps]
    TURN = STEPS - 3
    share = [min(UNITS, -(-UNITS * sum(width[:s]) // sum(width[:TURN]))) for s in range(STEPS + 1)]
    units_in = [range(share[s], share[s + 1]) for s in range(STEPS)]

    sums_of_block, place_of, pairs = [], {}, []
    for b in range(NB):
        first = TPB * b * (b + 1) // 2
        last, at = first + TPB * (b + 1) - 1, 0
        for a in range(first, last, 2):
            if a + 1 == last or (b == NB - 1 and a == last - 3):
                alone = [(a, 1), (a + 1, 1)]
            else:
                alone = [(a, 2)]
                pairs.append(a)
            for first_step, count in alone:
                at = max(at, first_step + (1 if count == 1 else 4))
                place_of[first_step] = at
                sums_of_block.append((b, first_step, count))
    sum_order = sorted(sums_of_block, key=lambda e: (place_of[e[1]], e[1]))
    SUMS = len(sum_order)
    sum_of_step = {a + i: n for n, (_, a, count) in enumerate(sum_order) for i in range(count)}
    last_sum = {b: max(n for n, e in enumerate(sum_order) if e[0] == b) for b in range(NB)}
    first_sum = {b: min(n for n, e in enumerate(sum_order) if e[0] == b) for b in range(NB)}

    def sums_in(s):
        return [n for n, e in enumerate(sum_order) if place_of[e[1]] == s]

    added = sem("c_added")
    sums_done = sem("c_sums_done")
    loaded, max_stored, buffer_free = sem("c_loaded"), sem("c_max_stored"), sem("c_buffer_free")
    unit_done, maxed, max_done = sem("c_unit_done"), sem("c_maxed"), sem("c_max_done")
    scores_done, exp_done, pv_done = sem("c_scores_done"), sem("c_exp_done"), sem("c_pv_done")
    ctx_read, sum_read, normed = sem("c_ctx_read"), sem("c_sum_read"), sem("c_normed")
    inverted, spread = sem("c_inverted"), sem("c_spread")
    v_product, v_done, values_ready = sem("c_v_product"), sem("c_v_done"), sem("c_values_ready")
    ctx_hi_done, ctx_lo_done, filled = sem("c_ctx_hi_done"), sem("c_ctx_lo_done"), sem("c_filled")
    S2_FREE, PROB_FREE, SUM_FREE, C_FREE, CN_FREE = 2, SUMS, 1, 2, 2

    with ExitStack() as ctx:
        sb = lambda n, s, d=F32: ctx.enter_context(nc.sbuf_tensor("c_" + n, s, d))
        ps = lambda n, s, d=F32: ctx.enter_context(nc.psum_tensor("c_" + n, s, d))
        Q, K = sb("q", [STACK + 1, 3, REP, T], F16), sb("k", [STACK + 1, 3, T], F16)
        V = sb("v", [P, NT, HD])
        PROB = sb("prob", [P, RING * REP, BANK])
        MAXES, NEGMAX = sb("maxes", [P, NT * REP, 2]), sb("negmax", [P, P])
        MROW = sb("mrow", [NT * REP, P], F16)
        C, R, CN = sb("c", [P, 2, BANK]), sb("r", [P, BANK]), sb("cn", [P, 2, BANK])
        ST, RT = sb("st", [P, BANK]), sb("rt", [P, BANK // HD])
        S1 = ps("s1", [P, 2, UNIT])
        S2 = ps("s2", [P, 2, BANK])
        CTX, SUM = ps("ctx", [P, BANK]), ps("sum", [P, BANK])
        block = ctx.enter_context(nc.Block())

        def diagonal(s):
            b, k = steps[s]
            return max(0, k - TPB * b) * P, k >= TPB * b

        @block.sync
        def _(sp):
            def load_group(g, buf):
                qrows, krows = bass.ds(g * P, P), bass.ds(D + g * HD, HD)
                for row, (qs, ks) in enumerate(((qk_hi, qk_hi), (qk_lo, qk_hi), (qk_hi, qk_lo))):
                    part = slice(row * HD, (row + 1) * HD)
                    sp.dma_start(Q[part, buf], qs[qrows, :].rearrange("(h d) t -> d h t", d=HD)
                                 ).then_inc(loaded, 16)
                    sp.dma_start(K[part, buf], ks[krows, :]).then_inc(loaded, 16)

            def store_maxima(g, buf):
                sp.wait_ge(maxed, SLOTS * g + SLOTS)
                sp.dma_start(Q[STACK:STACK + 1, buf].rearrange("o h (t q) -> o (h t) q", q=P),
                             MROW[:, :]).then_inc(max_stored, 16)
            load_group(0, 0)
            sp.wait_ge(loaded, 96)
            load_group(1, 1)
            store_maxima(0, 0)
            sp.wait_ge(loaded, 192)
            load_group(2, 2)
            store_maxima(1, 1)
            with sp.Fori(1, GROUPS - 2) as g:
                sp.wait_ge(loaded, 96 * g + 192)
                sp.sem_inc(buffer_free, 1)
                sp.wait_ge(scores_done, REP * STEPS * g)
                sp.sem_inc(buffer_free, 1)
                load_group(g + 2, (g + 2) % 3)
                store_maxima(g + 1, (g + 1) % 3)
            store_maxima(GROUPS - 1, (GROUPS - 1) % 3)

        def bodies(eng, body, ahead):
            ahead()
            with eng.Fori(0, GROUPS - 1) as g:
                body(g, True)
            body(GROUPS - 1, False)

        @block.tensor
        def _(pe):
            def unit(g, n):
                h, t, u = units[n]
                buf, slot = g % 3, n % 2
                free = SLOTS * g + (n - 1 if n else 0)
                if not (isinstance(free, int) and free <= 0):
                    pe.wait_ge(maxed, free)
                end = min(UNIT, (t + 1) * P - u * UNIT)
                for c in range(0, end, BANK):
                    n_c = min(BANK, end - c)
                    diag = u * UNIT + c + n_c == (t + 1) * P
                    last = nc.tensor.matmul(S1[:, slot, c:c + n_c], Q[0:STACK, buf, h, t * P:(t + 1) * P],
                                            K[0:STACK, buf, u * UNIT + c:u * UNIT + c + n_c],
                                            start=True, stop=not diag)
                    if diag:
                        last = nc.tensor.matmul(S1[:, slot, c + n_c - P:c + n_c], identb[:], causal[:],
                                                start=False, stop=True)
                last.then_inc(unit_done, 1)

            def turn_maxima(g):
                pe.wait_ge(max_done, g + 1)
                nc.tensor.transpose(S1[:, 0, 0:P], NEGMAX[:, :], ident[:]).then_inc(unit_done, 1)

            def scores(g, s, heads):
                b, k = steps[s]
                j, diag = diagonal(s)
                buf = g % 3
                for h in heads:
                    n = REP * STEPS * g + REP * s + h
                    pe.wait_ge(exp_done, n - 1 + S2_FREE)
                    last = nc.tensor.matmul(S2[:, h % 2, j:BANK], K[:, buf, k * P:(k + 1) * P],
                                            Q[:, buf, h, b * BANK + j:(b + 1) * BANK], start=True, stop=not diag)
                    if diag:
                        last = nc.tensor.matmul(S2[:, h % 2, j:j + P], causal[:], identb[:], start=False, stop=True)
                    last.then_inc(scores_done, 1)

            def products(g, s):
                b, k = steps[s]
                j, _ = diagonal(s)
                if s == 0:
                    pe.wait_ge(values_ready, g + 1)
                pe.wait_ge(exp_done, REP * STEPS * g + REP * s + REP + S2_FREE)
                if k == 0:
                    pe.wait_ge(ctx_read, NB * g + b + SUM_FREE)
                for h in range(REP):
                    last = nc.tensor.matmul(CTX[h * HD:(h + 1) * HD, j:BANK], V[:, k, :],
                                            PROB[:, REP * (s % RING) + h, j:BANK],
                                            start=(k == 0), stop=(k == TPB * (b + 1) - 1))
                last.then_inc(pv_done, 1)

            def sums(g, place):
                for n in sums_in(place):
                    b, s, count = sum_order[n]
                    j, _ = diagonal(s)
                    if n == first_sum[b]:
                        pe.wait_ge(sum_read, NB * g + b + SUM_FREE)
                    if count == 2:
                        pe.wait_ge(added, len(pairs) * g + pairs.index(s) + 1)
                    for h in range(REP):
                        last = nc.tensor.matmul(SUM[h * HD:(h + 1) * HD, j:BANK], ones[:],
                                                PROB[:, REP * (s % RING) + h, j:BANK],
                                                start=(n == first_sum[b]), stop=(n == last_sum[b]))
                    last.then_inc(sums_done, 1)

            def half_value_tile(i, half):
                if half == 0 and i >= 2:
                    pe.wait_ge(v_done, i - 1)
                KC = x_hi.shape[1]
                for k in range(half * KC // 2, (half + 1) * KC // 2):
                    xh, xl = (x[:, k, i * P:(i + 1) * P] for x in (x_hi, x_lo))
                    o = S2[:, i % 2, 0:VC]
                    nc.tensor.matmul(o, xh, wv_hi[:, k, :], start=(k == 0), stop=False)
                    nc.tensor.matmul(o, xh, wv_lo[:, k, :], start=False, stop=False)
                    last = nc.tensor.matmul(o, xl, wv_hi[:, k, :], start=False, stop=(k == KC - 1))
                if half:
                    last.then_inc(v_product, 1)

            def ahead():
                pe.sem_inc(sums_done, PROB_FREE)
                halves = [(i, half) for i in range(NT) for half in range(2)]
                for _ in range(2 * EARLY):
                    half_value_tile(*halves.pop(0))
                pe.wait_ge(loaded, 96)
                for n in range(UNITS):
                    unit(0, n)
                    if halves and n % PART == PART - 1:
                        half_value_tile(*halves.pop(0))
                turn_maxima(0)
                pe.wait_ge(v_done, NT)

            def body(g, first_pass):
                pe.wait_ge(max_stored, 16 * g + 16)
                if first_pass:
                    pe.wait_ge(loaded, 96 * g + 192)

                cut = (0, 4, 5, 8, 12)

                def some_units(s, part):
                    if first_pass:
                        n = units_in[s]
                        for i in n[-(-len(n) * cut[part] // 12):-(-len(n) * cut[part + 1] // 12)]:
                            unit(g + 1, i)
                for s in range(STEPS):
                    scores(g, s, (0,))
                    some_units(s, 0)
                    scores(g, s, (1,))
                    if s:
                        products(g, s - 1)
                    some_units(s, 1)
                    scores(g, s, (2,))
                    some_units(s, 2)
                    scores(g, s, (3,))
                    sums(g, s)
                    some_units(s, 3)
                    if first_pass and s == TURN:
                        turn_maxima(g + 1)
                products(g, STEPS - 1)
                sums(g, STEPS)
            bodies(pe, body, ahead)

        @block.scalar
        def _(act):
            act.sem_inc(exp_done, S2_FREE)
            act.sem_inc(ctx_read, SUM_FREE)
            for i in range(NT):
                act.wait_ge(v_product, i + 1)
                nc.scalar.activation(v_sb[:, i, :], S2[:, i % 2, 0:VC], ACT.Copy, scale=1.0 / (XS * WS)
                                     ).then_inc(v_done, 1)

            def read_context(g, b, s):
                act.wait_ge(pv_done, STEPS * g + s + 1)
                act.wait_ge(normed, NB * g + b - 1 + C_FREE)
                nc.scalar.activation(C[:, b % 2, :], CTX[:, :], ACT.Copy, scale=CS).then_inc(ctx_read, 1)
            with act.Fori(0, GROUPS) as g:
                for s in range(STEPS):
                    j, _ = diagonal(s)
                    before = sum_of_step[s - RING] + SUMS if s >= RING else sum_of_step[s - RING + STEPS]
                    act.wait_ge(sums_done, SUMS * g + before + 1)
                    for h in range(REP):
                        act.wait_ge(scores_done, REP * STEPS * g + REP * s + h + 1)
                        nc.scalar.activation(PROB[:, REP * (s % RING) + h, j:BANK], S2[:, h % 2, j:BANK], ACT.Exp,
                                             scale=exp_scale).then_inc(exp_done, 1)
                    if s - 1 in last_of:
                        read_context(g, last_of[s - 1], s - 1)
                read_context(g, NB - 1, STEPS - 1)

        @block.vector
        def _(dve):
            def unit(g, n):
                h, t, u = units[n]
                end = min(UNIT, (t + 1) * P - u * UNIT)
                dve.wait_ge(unit_done, SLOTS * g + n + 1)
                nc.vector.tensor_reduce(MAXES[:, h * NT + t, u:u + 1], S1[:, n % 2, 0:end],
                                        AX.X, ALU.max).then_inc(maxed, 1)

            def join_maxima(g):
                dve.wait_ge(maxed, SLOTS * g + UNITS)
                nc.vector.tensor_reduce(NEGMAX[:, 0:NT * REP], MAXES[:, :, :], AX.X, ALU.max, negate=True
                                        ).then_inc(max_done, 1)

            def write_maxima(g):
                if not (isinstance(g, int) and g == 0):
                    dve.wait_ge(max_stored, 16 * g)
                dve.wait_ge(unit_done, SLOTS * g + SLOTS)
                nc.vector.tensor_scalar(MROW[:, :], S1[0:NT * REP, 0, 0:P], 1.0 / MS, None, ALU.mult
                                        ).then_inc(maxed, 1)

            def ahead():
                dve.sem_inc(sum_read, SUM_FREE)
                dve.sem_inc(normed, C_FREE)
                nc.vector.memset(MAXES[:], LEAST)
                nc.vector.memset(NEGMAX[:], 0.0)
                nc.vector.memset(K[STACK:STACK + 1, :, :], MS).then_inc(filled, 1)
                dve.wait_ge(filled, 1)
                for n in range(UNITS):
                    unit(0, n)
                join_maxima(0)
                write_maxima(0)

            PIECES = 3

            def invert_piece(g, b, i):
                n = NB * g + b
                if i == 0:
                    dve.wait_ge(sums_done, SUMS * g + last_sum[b] + 1 + PROB_FREE)
                    nc.vector.transpose(ST[:, :], SUM[:, :]).then_inc(sum_read, 1)
                elif i == 1:
                    dve.wait_ge(sum_read, n + 1 + SUM_FREE)
                    nc.vector.reciprocal(RT[:, :], ST[:, 0:BANK:HD]).then_inc(inverted, 1)
                else:
                    dve.wait_ge(inverted, n + 1)
                    dve.wait_ge(normed, n + C_FREE)
                    nc.vector.transpose(R[:, :], RT[:].rearrange("p (c o) -> p c o", o=1)
                                        .broadcast_to([P, BANK // HD, HD])).then_inc(spread, 1)

            def normalise(g, b):
                n = NB * g + b
                dve.wait_ge(ctx_lo_done, n - 1 + CN_FREE)
                dve.wait_ge(ctx_read, n + 1 + SUM_FREE)
                dve.wait_ge(spread, n + 1)
                nc.vector.tensor_tensor(CN[:, b % 2, :], C[:, b % 2, :], R[:], ALU.mult).then_inc(normed, 1)

            def body(g, first_pass, first_group):
                left = [] if first_group else [(g - 1, NB - 1, i) for i in range(PIECES + 1)]

                def one_piece():
                    if left:
                        of, b, i = left.pop(0)
                        if i < PIECES:
                            invert_piece(of, b, i)
                        else:
                            normalise(of, b)
                if first_pass:
                    dve.wait_ge(max_done, g + 1)
                for s in range(STEPS):
                    if s - 2 in last_of:
                        left += [(g, last_of[s - 2], i) for i in range(PIECES + 1)]
                    one_piece()
                    if first_pass:
                        for n in units_in[s]:
                            unit(g + 1, n)
                            if n == UNITS - 1:
                                join_maxima(g + 1)
                        if s == TURN:
                            write_maxima(g + 1)
                assert not left
            ahead()
            body(0, True, True)
            with dve.Fori(1, GROUPS - 1) as g:
                body(g, True, False)
            body(GROUPS - 1, False, False)
            for i in range(PIECES):
                invert_piece(GROUPS - 1, NB - 1, i)
            normalise(GROUPS - 1, NB - 1)

        @block.gpsimd
        def _(pool):
            def take_values(g):
                nc.gpsimd.tensor_copy(V[:, :, :], v_sb[:, :, bass.ds(g * HD, HD)]).then_inc(values_ready, 1)

            def cut_context(g, b):
                n = NB * g + b
                at = slice(b * BANK, (b + 1) * BANK)
                pool.wait_ge(normed, n + 1 + C_FREE)
                nc.gpsimd.tensor_copy(c_hi[:, g, at], CN[:, b % 2, :]).then_inc(ctx_hi_done, 1)
                pool.wait_ge(ctx_hi_done, n + 1)
                nc.gpsimd.tensor_tensor(c_lo[:, g, at], CN[:, b % 2, :], c_hi[:, g, at], ALU.subtract
                                        ).then_inc(ctx_lo_done, 1)

            def add_pair(g, n):
                a = pairs[n]
                j, _ = diagonal(a + 1)
                pool.wait_ge(pv_done, STEPS * g + a + 1)
                pool.wait_ge(exp_done, REP * (STEPS * g + a + 2) + S2_FREE)
                for h in range(REP):
                    one, two = (PROB[:, REP * (t % RING) + h, j:BANK] for t in (a, a + 1))
                    last = nc.gpsimd.tensor_tensor(one, one, two, ALU.add)
                last.then_inc(added, 1)
            pool.sem_inc(ctx_lo_done, CN_FREE)
            pool.wait_ge(v_done, NT)
            take_values(0)

            def body(g, first_group):
                cuts = {}
                for b in range(NB - 1):
                    last = TPB * (b + 1) * (b + 2) // 2 - 1
                    cuts[min(a for a in pairs if a >= last + 5)] = (g, b)
                for n, a in enumerate(pairs):
                    if a in cuts:
                        cut_context(*cuts[a])
                    add_pair(g, n)
                    if n == 0 and not first_group:
                        cut_context(g - 1, NB - 1)
                pool.wait_ge(pv_done, STEPS * g + STEPS)
                take_values((g + 1) % GROUPS)
            body(0, True)
            with pool.Fori(1, GROUPS) as g:
                body(g, False)
            cut_context(GROUPS - 1, NB - 1)


def project_context(nc, c_hi, c_lo, wo, bo, x, x1_dram, ident, x2_hi, x2_lo, sem):
    KC, T = c_hi.shape[1], c_hi.shape[2]
    D = KC * P
    PAIRS = T // P // 2
    wo_loaded, bo_loaded = [sem(f"d_wo_loaded{k}") for k in range(KC)], sem("d_bo_loaded")
    wo_cut_hi, wo_cut_lo = sem("d_wo_cut_hi"), sem("d_wo_cut_lo")
    x_loaded, x1_stored = [sem(f"d_x_loaded{s}") for s in range(2)], [sem(f"d_x1_stored{s}") for s in range(2)]
    y_product, y_read, y_normed, x1_done = sem("d_y_product"), sem("d_y_read"), sem("d_y_normed"), sem("d_x1_done")
    norm_done, turned, hi_done, lo_done = sem("d_norm_done"), sem("d_turned"), sem("d_hi_done"), sem("d_lo_done")
    with ExitStack() as ctx:
        sb = lambda n, s, d=F32: ctx.enter_context(nc.sbuf_tensor("d_" + n, s, d))
        WO, BO = sb("wo", [P, 2, D]), sb("bo", [P, D])
        wo_hi, wo_lo = sb("wo_hi", [P, KC, D], F16), sb("wo_lo", [P, KC, D], F16)
        X, Y, X1, XN = (sb(n, [P, 2, D]) for n in ("x", "y", "x1", "xn"))
        y_norm = RowNorm(nc, ctx, sem, "d_y_norm", 1.0, 1.0)
        x_norm = RowNorm(nc, ctx, sem, "d_x_norm", 1.0, XS)
        YP = ctx.enter_context(nc.psum_tensor("d_yp", [P, 2, D], F32))
        XT = ctx.enter_context(nc.psum_tensor("d_xt", [P, 2, D], F32))
        raw = [t[:, s, :] for t in (WO, XN, X1, Y) for s in range(2)]
        assert len(raw) == KC
        block = ctx.enter_context(nc.Block())

        def tokens(i, s):
            return bass.ds((2 * i + s) * P, P)

        @block.sync
        def _(sp):
            def load_rows(i):
                for s in range(2):
                    sp.dma_start(X[:, s, :], x[tokens(i, s), :]).then_inc(x_loaded[s], 16)

            def store_rows(i):
                for s in range(2):
                    sp.wait_ge(x1_done, 2 * i + s + 1)
                    sp.dma_start(x1_dram[tokens(i, s), :], X1[:, s, :]).then_inc(x1_stored[s], 16)
            for k in range(KC):
                sp.dma_start(raw[k], wo[k * P:(k + 1) * P, :]).then_inc(wo_loaded[k], 16)
            sp.dma_start(BO[:], bo.rearrange("(o n) -> o n", o=1).broadcast_to([P, D])).then_inc(bo_loaded, 16)
            load_rows(0)
            with sp.Fori(0, PAIRS - 1) as i:
                store_rows(i)
                load_rows(i + 1)
            store_rows(PAIRS - 1)
            for s in range(2):
                sp.wait_ge(x1_stored[s], 16 * PAIRS)

        @block.tensor
        def _(pe):
            def product_chunk(i, s, k):
                ch, cl = (c[:, k, tokens(i, s)] for c in (c_hi, c_lo))
                for stat, w, a, z in ((ch, wo_hi, 1, 0), (ch, wo_lo, 0, 0), (cl, wo_hi, 0, 1)):
                    for n in range(0, D, BANK):
                        last = nc.tensor.matmul(YP[:, s, n:n + BANK], stat, w[:, k, n:n + BANK],
                                                start=(k == 0 and a == 1), stop=(k == KC - 1 and z == 1))
                return last

            def product(i, s):
                pe.wait_ge(y_read, 2 * i + s - 1)
                for k in range(KC):
                    last = product_chunk(i, s, k)
                last.then_inc(y_product, 1)

            def turn(i):
                for s in range(2):
                    pe.wait_ge(norm_done, 2 * i + s + 1)
                    for c in range(KC):
                        last = nc.tensor.transpose(XT[:, s, c * P:(c + 1) * P], XN[:, s, c * P:(c + 1) * P],
                                                   ident[:])
                    last.then_inc(turned, 1)
            for k in range(KC):
                pe.wait_ge(wo_cut_lo, k + 1)
                for s in range(2):
                    last = product_chunk(0, s, k)
                    if k == KC - 1:
                        last.then_inc(y_product, 1)
            product(1, 0)
            product(1, 1)
            with pe.Fori(2, PAIRS) as i:
                product(i, 0)
                turn(i - 2)
                product(i, 1)
            turn(PAIRS - 2)
            turn(PAIRS - 1)

        @block.vector
        def _(dve):
            def read_product(i, s):
                dve.wait_ge(y_product, 2 * i + s + 1)
                nc.vector.scalar_tensor_tensor(Y[:, s, :], YP[:, s, :], 1.0 / (CS * WS), BO[:],
                                               ALU.mult, ALU.add).then_inc(y_read, 1)

            def cut_turned(i):
                for s in range(2):
                    dve.wait_ge(hi_done, 2 * i + s + 1)
                    nc.vector.tensor_tensor(x2_lo[:, :, tokens(i, s)], XT[:, s, :].rearrange("p (c t) -> p c t", t=P),
                                            x2_hi[:, :, tokens(i, s)], ALU.subtract).then_inc(lo_done, 1)

            def body(i, first=False, last=False):
                read_product(i, 1)
                y_norm.on_vector(dve, i, lambda s: dve.wait_ge(y_read, 2 * i + s + 1),
                                 lambda s: Y[:, s, :], lambda s: Y[:, s, :], y_normed)
                if not first:
                    cut_turned(i - 1)
                if not last:
                    dve.wait_ge(x1_done, 2 * i + 1)
                    read_product(i + 1, 0)
                x_norm.on_vector(dve, i, lambda s: dve.wait_ge(x1_done, 2 * i + s + 1),
                                 lambda s: X1[:, s, :], lambda s: XN[:, s, :], norm_done)
            for k in range(KC):
                dve.wait_ge(wo_cut_hi, k + 1)
                nc.vector.scalar_tensor_tensor(wo_lo[:, k, :], raw[k], WS, wo_hi[:, k, :],
                                               ALU.mult, ALU.subtract).then_inc(wo_cut_lo, 1)
            dve.wait_ge(bo_loaded, 16)
            read_product(0, 0)
            body(0, first=True)
            with dve.Fori(1, PAIRS - 1) as i:
                body(i)
            body(PAIRS - 1, last=True)
            cut_turned(PAIRS - 1)

        @block.scalar
        def _(act):
            def cut_turned(i):
                for s in range(2):
                    act.wait_ge(turned, 2 * i + s + 1)
                    nc.scalar.activation(x2_hi[:, :, tokens(i, s)], XT[:, s, :].rearrange("p (c t) -> p c t", t=P),
                                         ACT.Copy).then_inc(hi_done, 1)
            for k in range(KC):
                act.wait_ge(wo_loaded[k], 16)
                nc.scalar.activation(wo_hi[:, k, :], raw[k], ACT.Copy, scale=WS).then_inc(wo_cut_hi, 1)
            y_norm.on_scalar(act, 0)
            x_norm.on_scalar(act, 0)
            with act.Fori(1, PAIRS) as i:
                y_norm.on_scalar(act, i)
                cut_turned(i - 1)
                x_norm.on_scalar(act, i)
            cut_turned(PAIRS - 1)

        @block.gpsimd
        def _(pool):
            def residual(i, first):
                for s in range(2):
                    if not first:
                        pool.wait_ge(x1_stored[s], 16 * i)
                    pool.wait_ge(x_loaded[s], 16 * i + 16)
                    pool.wait_ge(y_normed, 2 * i + s + 1)
                    nc.gpsimd.tensor_tensor(X1[:, s, :], X[:, s, :], Y[:, s, :], ALU.add).then_inc(x1_done, 1)
            residual(0, True)
            with pool.Fori(1, PAIRS) as i:
                residual(i, False)


def gate_and_up(nc, x2_hi, x2_lo, quantised, ident, wd_hi, wd_lo, h_hi, h_lo, sem):
    KC, T = x2_hi.shape[1], x2_hi.shape[2]
    D = KC * P
    NB = T // BANK
    gate_q, up_q, down_q = (packed for packed, _, _ in quantised)
    inter = gate_q.shape[0]
    FULL, REST = inter // P, inter % P
    CHUNKS = FULL + (REST > 0)
    assert CHUNKS % 2 == 0 and 0 < REST and REST % QGROUP == 0 and NB == 4
    GROUPS_IN, GROUPS_MID = D // QGROUP, inter // QGROUP
    GATE, UP, DOWN = range(3)
    in_scale = 1.0 / (XS * WS)

    tables_loaded = [sem(f"e_{n}_tables_loaded") for n in ("gate", "up", "down")]
    raw_loaded = [sem(f"e_raw_loaded{s}") for s in range(2)]
    unpacked, shifted, scaled = sem("e_unpacked"), sem("e_shifted"), sem("e_scaled")
    turned, cut_hi, cut_lo = sem("e_turned"), sem("e_cut_hi"), sem("e_cut_lo")
    gate_product, up_product, silu_done = sem("e_gate_product"), sem("e_up_product"), sem("e_silu_done")
    h_done, hi_done, lo_done, cleared = (sem(f"e_{n}") for n in ("h_done", "hi_done", "lo_done", "cleared"))
    hi_stored, lo_stored = ([sem(f"e_{n}_stored{s}") for s in range(2)] for n in ("hi", "lo"))
    FREE = 2

    with ExitStack() as ctx:
        sb = lambda n, s, d=F32: ctx.enter_context(nc.sbuf_tensor("e_" + n, s, d))
        scales = [sb(f"{n}_s", [P, CHUNKS, GROUPS_IN]) for n in ("gate", "up")] + [sb("down_s", [P, KC, GROUPS_MID])]
        zeros = [sb(f"{n}_z", [P, CHUNKS, GROUPS_IN]) for n in ("gate", "up")] + [sb("down_z", [P, KC, GROUPS_MID])]
        RAW, NIBBLES = sb("raw", [P, 2, D // 2], I32), sb("nibbles", [P, D], I32)
        W = sb("w", [P, 2, D])
        w_hi, w_lo = (sb(n, [P, 2, 2, KC, P], F16) for n in ("w_hi", "w_lo"))
        SILU, H = sb("silu", [P, 2, BANK]), sb("h", [P, 2, BANK])
        HH, HL = sb("hh", [P, 2, BANK], F16), sb("hl", [P, 2, BANK], F16)
        WT = ctx.enter_context(nc.psum_tensor("e_wt", [P, 2, D], F32))
        GP = ctx.enter_context(nc.psum_tensor("e_gp", [P, 2, BANK], F32))
        UP_ = ctx.enter_context(nc.psum_tensor("e_up", [P, 2, BANK], F32))
        block = ctx.enter_context(nc.Block())

        def number(chunk):
            return 2 * chunk[0] + chunk[1]

        def height(chunk):
            c = number(chunk)
            return REST if isinstance(c, int) and c == FULL else P

        def after(chunk):
            j, parity = chunk
            return (j, 1) if parity == 0 else (j + 1, 0)

        def weights(chunk, kind):
            j, parity = chunk
            return 6 * j + 3 * parity + kind, (parity + kind) % 2

        def wait_positive(eng, signal, value):
            if not (isinstance(value, int) and value <= 0):
                eng.wait_ge(signal, value)

        def extent(kind, chunk):
            n = height(chunk)
            return (P, KC * n // 2) if kind == DOWN else (n, D // 2)

        def table(t, kind, chunk):
            n = height(chunk)
            if kind != DOWN:
                return t[kind][0:n, number(chunk), :].unsqueeze(2).broadcast_to([n, GROUPS_IN, QGROUP])
            at = bass.ds(number(chunk) * (P // QGROUP), n // QGROUP)
            return t[kind][:, :, at].unsqueeze(3).broadcast_to([P, KC, n // QGROUP, QGROUP])

        def grouped(ap, kind, chunk):
            rows, packed = extent(kind, chunk)
            flat = ap[0:rows, 0:2 * packed]
            if kind != DOWN:
                return flat.rearrange("p (g j) -> p g j", j=QGROUP)
            return flat.rearrange("p (k g j) -> p k g j", k=KC, j=QGROUP)

        def turned_parts(kind, chunk):
            n, (_, slot) = height(chunk), weights(chunk, kind)
            if kind == DOWN:
                return WT[0:n, slot, :], wd_hi[0:n, number(chunk), :], wd_lo[0:n, number(chunk), :]
            at = (slice(None), kind, chunk[1], slice(None), slice(0, n))
            return WT[:, slot, :].rearrange("p (k i) -> p k i", i=P)[:, :, 0:n], w_hi[at], w_lo[at]

        def aside(chunk, coming, b):
            if b == 0:
                return [(chunk, DOWN)]
            return [(coming, b - 1)] if coming and b < 3 else []

        def all_chunks(eng, prepare, multiply, tables):
            for step in prepare if isinstance(prepare, tuple) else (prepare,):
                for kind in (GATE, UP):
                    tables(kind)
                    step((0, 0), kind)
            tables(DOWN)
            with eng.Fori(0, FULL // 2) as j:
                for parity in range(2):
                    multiply((j, parity), after((j, parity)))
            multiply((FULL // 2, 0), (FULL // 2, 1))
            multiply((FULL // 2, 1), None)

        @block.sync
        def _(sp):
            def load_tables(kind):
                for buf, src in ((zeros[kind], quantised[kind][2]), (scales[kind], quantised[kind][1])):
                    if kind == DOWN:
                        sp.dma_start(buf[:], src.rearrange("(k p) g -> p k g", p=P)).then_inc(tables_loaded[kind], 16)
                    else:
                        sp.dma_start(buf[:, 0:FULL, :], src[0:FULL * P, :].rearrange("(c p) g -> p c g", p=P)
                                     ).then_inc(tables_loaded[kind], 16)
                        sp.dma_start(buf[0:REST, FULL, :], src[FULL * P:, :]).then_inc(tables_loaded[kind], 16)
            for s in range(2):
                sp.sem_inc(hi_stored[s], 16)
                sp.sem_inc(lo_stored[s], 16)

            def load(chunk, kind):
                m, slot = weights(chunk, kind)
                n, c = height(chunk), number(chunk)
                rows, packed = extent(kind, chunk)
                wait_positive(sp, unpacked, m - 1)
                if kind == DOWN:
                    dst = RAW[:, slot, 0:packed].rearrange("p (k i) -> p k i", k=KC)
                    src = down_q[:, bass.ds(c * (P // 2), n // 2)].rearrange("(k p) i -> p k i", p=P)
                else:
                    dst, src = RAW[0:n, slot, :], (gate_q, up_q)[kind][bass.ds(c * P, n), :]
                sp.dma_start(dst, src).then_inc(raw_loaded[slot], 16)

            def multiply(chunk, coming):
                c, n = number(chunk), height(chunk)
                for b in range(NB):
                    if coming and b < 3:
                        load(coming, b)
                    for buf, done, dram, stored in ((HH, hi_done, h_hi, hi_stored), (HL, lo_done, h_lo, lo_stored)):
                        sp.wait_ge(done, NB * c + b + 1 + (FREE if done is lo_done else 0))
                        sp.dma_start(dram[bass.ds(c * P, n), b * BANK:(b + 1) * BANK], buf[0:n, b % 2, :]
                                     ).then_inc(stored[b % 2], 16)

            def tables(kind):
                load_tables(kind)
                if kind == DOWN:
                    load((0, 0), DOWN)
            all_chunks(sp, load, multiply, tables)
            for s in range(2):
                sp.wait_ge(hi_stored[s], 16 * (NB // 2 * CHUNKS + 1))
                sp.wait_ge(lo_stored[s], 16 * (NB // 2 * CHUNKS + 1))

        @block.tensor
        def _(pe):
            def prepare(chunk, kind):
                m, slot = weights(chunk, kind)
                n = height(chunk)
                wait_positive(pe, cut_lo, m - 1)
                pe.wait_ge(scaled, m + 1)
                for k in range(KC):
                    if kind == DOWN:
                        last = nc.tensor.transpose(WT[0:n, slot, k * P:(k + 1) * P], W[:, slot, k * n:(k + 1) * n],
                                                   ident[:])
                    else:
                        last = nc.tensor.transpose(WT[:, slot, k * P:k * P + n], W[0:n, slot, k * P:(k + 1) * P],
                                                   ident[0:n, 0:n])
                last.then_inc(turned, 1)

            def multiply(chunk, coming):
                c, n, parity = number(chunk), height(chunk), chunk[1]
                for b in range(NB):
                    if b == 0:
                        pe.wait_ge(cut_lo, 6 * chunk[0] + 3 * parity + 2)
                    pe.wait_ge(h_done, NB * c + b - 1 + FREE)
                    tok = slice(b * BANK, (b + 1) * BANK)
                    for kind, out, done in ((GATE, GP, gate_product), (UP, UP_, up_product)):
                        o = out[0:n, b % 2, :]
                        for k in range(KC):
                            wh, wl = (w[:, kind, parity, k, 0:n] for w in (w_hi, w_lo))
                            nc.tensor.matmul(o, wh, x2_hi[:, k, tok], start=(k == 0), stop=False)
                            nc.tensor.matmul(o, wh, x2_lo[:, k, tok], start=False, stop=False)
                            last = nc.tensor.matmul(o, wl, x2_hi[:, k, tok], start=False, stop=(k == KC - 1))
                        last.then_inc(done, 1)
                    for of, kind in aside(chunk, coming, b):
                        prepare(of, kind)
            all_chunks(pe, prepare, multiply, lambda kind: None)

        @block.vector
        def _(dve):
            dve.sem_inc(h_done, FREE)

            def unpack(chunk, kind):
                m, slot = weights(chunk, kind)
                rows, packed = extent(kind, chunk)
                wait_positive(dve, shifted, m)
                dve.wait_ge(raw_loaded[slot], 16 * (3 * chunk[0] + (3 * chunk[1] + kind) // 2 + 1))
                raw = RAW[0:rows, slot, 0:packed]
                pair = NIBBLES[0:rows, 0:2 * packed].rearrange("p (j two) -> p two j", two=2)
                nc.vector.tensor_scalar(pair[:, 0, :], raw, 4, 15, ALU.logical_shift_right, ALU.bitwise_and)
                nc.vector.tensor_scalar(pair[:, 1, :], raw, 15, None, ALU.bitwise_and).then_inc(unpacked, 1)
                wait_positive(dve, turned, m - 1)
                dve.wait_ge(unpacked, m + 1)
                nc.vector.tensor_tensor(grouped(W[:, slot], kind, chunk), grouped(NIBBLES, kind, chunk),
                                        table(zeros, kind, chunk), ALU.subtract).then_inc(shifted, 1)

            def cut(chunk, kind):
                m, _ = weights(chunk, kind)
                psum, hi, lo = turned_parts(kind, chunk)
                dve.wait_ge(cut_hi, m + 1)
                nc.vector.scalar_tensor_tensor(lo, psum, WS, hi, ALU.mult, ALU.subtract).then_inc(cut_lo, 1)

            def multiply(chunk, coming):
                c, n = number(chunk), height(chunk)
                for b in range(NB):
                    for of, kind in aside(chunk, coming, b):
                        unpack(of, kind)
                    dve.wait_ge(lo_done, NB * c + b - 1 + FREE)
                    dve.wait_ge(silu_done, NB * c + b + 1)
                    dve.wait_ge(up_product, NB * c + b + 1)
                    nc.vector.scalar_tensor_tensor(H[0:n, b % 2, :], UP_[0:n, b % 2, :], HS * in_scale,
                                                   SILU[0:n, b % 2, :], ALU.mult, ALU.mult).then_inc(h_done, 1)
                    for of, kind in aside(chunk, coming, b):
                        cut(of, kind)
            all_chunks(dve, (unpack, cut), multiply, lambda kind: dve.wait_ge(tables_loaded[kind], 32 if kind == DOWN else 64))

        @block.scalar
        def _(act):
            def prepare(chunk, kind):
                m, _ = weights(chunk, kind)
                psum, hi, lo = turned_parts(kind, chunk)
                act.wait_ge(turned, m + 1)
                nc.scalar.activation(hi, psum, ACT.Copy, scale=WS).then_inc(cut_hi, 1)

            def multiply(chunk, coming):
                c, n = number(chunk), height(chunk)
                for b in range(NB):
                    act.wait_ge(gate_product, NB * c + b + 1)
                    nc.scalar.activation(SILU[0:n, b % 2, :], GP[0:n, b % 2, :], ACT.Silu, scale=in_scale
                                         ).then_inc(silu_done, 1)
                    act.wait_ge(hi_stored[b % 2], 16 * (NB // 2 * c + b // 2 + 1))
                    act.wait_ge(lo_done, NB * c + b - 1 + FREE)
                    act.wait_ge(h_done, NB * c + b + 1 + FREE)
                    nc.scalar.activation(HH[0:n, b % 2, :], H[0:n, b % 2, :], ACT.Copy).then_inc(hi_done, 1)
                    for of, kind in aside(chunk, coming, b):
                        prepare(of, kind)
            all_chunks(act, prepare, multiply, lambda kind: None)

        @block.gpsimd
        def _(pool):
            pool.sem_inc(lo_done, FREE)
            for w in (wd_hi, wd_lo):
                last = nc.gpsimd.memset(w[REST:P, FULL, :], 0.0)
            last.then_inc(cleared, 1)
            pool.wait_ge(cleared, 1)

            def prepare(chunk, kind):
                m, slot = weights(chunk, kind)
                pool.wait_ge(shifted, m + 1)
                nc.gpsimd.tensor_tensor(grouped(W[:, slot], kind, chunk), grouped(W[:, slot], kind, chunk),
                                        table(scales, kind, chunk), ALU.mult).then_inc(scaled, 1)

            def multiply(chunk, coming):
                c, n = number(chunk), height(chunk)
                for b in range(NB):
                    for of, kind in aside(chunk, coming, b):
                        prepare(of, kind)
                    pool.wait_ge(lo_stored[b % 2], 16 * (NB // 2 * c + b // 2 + 1))
                    pool.wait_ge(hi_done, NB * c + b + 1)
                    nc.gpsimd.tensor_tensor(HL[0:n, b % 2, :], H[0:n, b % 2, :], HH[0:n, b % 2, :], ALU.subtract
                                            ).then_inc(lo_done, 1)
            all_chunks(pool, prepare, multiply, lambda kind: pool.wait_ge(tables_loaded[kind], 32 if kind == DOWN else 64))


def project_down(nc, h_hi, h_lo, wd_hi, wd_lo, x1_dram, out, sem):
    CHUNKS, D = wd_hi.shape[1], wd_hi.shape[2]
    inter, T = h_hi.shape
    FULL, REST = inter // P, inter % P
    BLOCK = 2 * P
    ROUNDS = T // BLOCK // 2
    h_loaded = [sem(f"f_h_loaded{u}") for u in range(2)]
    part_loaded = [sem(f"f_part_loaded{part}") for part in range(2)]
    HALF = CHUNKS // 2
    x_loaded = [sem(f"f_x_loaded{u}") for u in range(2)]
    stored = [sem(f"f_stored{u}") for u in range(2)]
    product, normed, added, cleared = sem("f_product"), sem("f_normed"), sem("f_added"), sem("f_cleared")
    with ExitStack() as ctx:
        sb = lambda n, s, d=F32: ctx.enter_context(nc.sbuf_tensor("f_" + n, s, d))
        H_HI, H_LO = (sb(n, [P, 2, CHUNKS, BLOCK], F16) for n in ("h_hi", "h_lo"))
        X = sb("x", [P, 2, 2, D])
        Z = sb("z", [P, 2, 2, D])
        norm = RowNorm(nc, ctx, sem, "f_norm", HS * WS, 1.0)
        YP = ctx.enter_context(nc.psum_tensor("f_yp", [P, 2, 2, D], F32))
        block = ctx.enter_context(nc.Block())

        def rows(i, u):
            return bass.ds((2 * i + u) * BLOCK, BLOCK)

        @block.sync
        def _(sp):
            def load_first():
                for part, at in enumerate((slice(0, HALF), slice(HALF, FULL))):
                    for buf, src in ((H_HI, h_hi), (H_LO, h_lo)):
                        sp.dma_start(buf[:, 0, at, :], src[at.start * P:at.stop * P, rows(0, 0)]
                                     .rearrange("(c p) t -> p c t", p=P)).then_inc(part_loaded[part], 16)
                        if part:
                            sp.dma_start(buf[0:REST, 0, FULL, :], src[FULL * P:, rows(0, 0)]
                                         ).then_inc(part_loaded[part], 16)
                sp.dma_start(X[:, 0], x1_dram[rows(0, 0), :].rearrange("(s p) d -> p s d", p=P)
                             ).then_inc(x_loaded[0], 16)

            def load(i, u):
                for buf, src in ((H_HI, h_hi), (H_LO, h_lo)):
                    sp.dma_start(buf[:, u, 0:FULL, :], src[0:FULL * P, rows(i, u)].rearrange("(c p) t -> p c t", p=P)
                                 ).then_inc(h_loaded[u], 16)
                    sp.dma_start(buf[0:REST, u, FULL, :], src[FULL * P:, rows(i, u)]).then_inc(h_loaded[u], 16)
                sp.dma_start(X[:, u], x1_dram[rows(i, u), :].rearrange("(s p) d -> p s d", p=P)
                             ).then_inc(x_loaded[u], 16)

            def store(i, u):
                sp.wait_ge(added, 4 * i + 2 * u + 2)
                sp.dma_start(out[rows(i, u), :].rearrange("(s p) d -> p s d", p=P), Z[:, u]).then_inc(stored[u], 16)
            load_first()
            load(0, 1)
            with sp.Fori(0, ROUNDS - 1) as i:
                for u in range(2):
                    store(i, u)
                    load(i + 1, u)
            for u in range(2):
                store(ROUNDS - 1, u)
            for u in range(2):
                sp.wait_ge(stored[u], 16 * ROUNDS)

        @block.tensor
        def _(pe):
            pe.wait_ge(cleared, 1)

            def block_product(i, u, first):
                if not (first and u == 0):
                    pe.wait_ge(h_loaded[u], 64 * i + 64 * u)
                for s in range(2):
                    if not first:
                        pe.wait_ge(normed, 4 * i + 2 * u + s - 3)
                    for c in range(CHUNKS):
                        if first and u == 0 and s == 0 and c in (0, HALF):
                            pe.wait_ge(part_loaded[c // HALF], 64 if c else 32)
                        hh, hl = (h[:, u, c, s * P:(s + 1) * P] for h in (H_HI, H_LO))
                        for stat, w, a, z in ((hh, wd_hi, 1, 0), (hh, wd_lo, 0, 0), (hl, wd_hi, 0, 1)):
                            for n in range(0, D, BANK):
                                last = nc.tensor.matmul(YP[:, u, s, n:n + BANK], stat, w[:, c, n:n + BANK],
                                                        start=(c == 0 and a == 1), stop=(c == CHUNKS - 1 and z == 1))
                    last.then_inc(product, 1)
            block_product(0, 0, True)
            block_product(0, 1, True)
            with pe.Fori(1, ROUNDS) as i:
                for u in range(2):
                    block_product(i, u, False)

        @block.vector
        def _(dve):
            def normalise(i, u, first):
                if not first:
                    dve.wait_ge(stored[u], 16 * i)
                norm.on_vector(dve, 2 * i + u, lambda s: dve.wait_ge(product, 4 * i + 2 * u + s + 1),
                               lambda s: YP[:, u, s, :], lambda s: Z[:, u, s, :], normed)
            normalise(0, 0, True)
            normalise(0, 1, True)
            with dve.Fori(1, ROUNDS) as i:
                for u in range(2):
                    normalise(i, u, False)

        @block.scalar
        def _(act):
            with act.Fori(0, 2 * ROUNDS) as r:
                norm.on_scalar(act, r)

        @block.gpsimd
        def _(pool):
            for h in (H_HI, H_LO):
                last = nc.gpsimd.memset(h[REST:P, :, FULL, :], 0.0)
            last.then_inc(cleared, 1)
            pool.wait_ge(cleared, 1)
            with pool.Fori(0, ROUNDS) as i:
                for u in range(2):
                    pool.wait_ge(x_loaded[u], 16 * i + 16)
                    for s in range(2):
                        pool.wait_ge(normed, 4 * i + 2 * u + s + 1)
                        nc.gpsimd.tensor_tensor(Z[:, u, s, :], X[:, u, s, :], Z[:, u, s, :], ALU.add
                                                ).then_inc(added, 1)


def sandwich_layer(nc, x, wq, wkv, wo, bo, gate_q, up_q, down_q, gate_s, gate_z, up_s, up_z,
                   down_s, down_z, out):
    T, D = x.shape
    NT, KC = T // P, D // P
    VC = wkv.shape[1] // 2
    QK = D + VC
    inter = gate_q.shape[0]
    qk_hi, qk_lo = (nc.dram_tensor(n, (QK, T), F16).ap() for n in ("qk_hi", "qk_lo"))
    h_hi, h_lo = (nc.dram_tensor(n, (inter, T), F16).ap() for n in ("h_hi", "h_lo"))
    x1_dram = nc.dram_tensor("x1_dram", (T, D), F32).ap()
    with ExitStack() as whole:
        def sem(name):
            return whole.enter_context(nc.semaphore(name))

        def tensor(stack, name, shape, dtype, side="left"):
            return stack.enter_context(nc.sbuf_tensor(name, shape, dtype, side=side))
        ident, identb = tensor(whole, "ident", [P, P], F32), tensor(whole, "identb", [P, P], BF16)
        causal, ones = tensor(whole, "causal", [P, P], BF16), tensor(whole, "ones", [P, D // HEADS], F32)
        build_constants(nc, ident, identb, causal, ones, sem)
        with ExitStack() as context:
            c_hi, c_lo = (tensor(context, n, [P, KC, T], F16) for n in ("c_hi", "c_lo"))
            with ExitStack() as attention:
                v_sb = tensor(attention, "v_sb", [P, NT, VC], F32, "right")
                wv_hi, wv_lo = (tensor(attention, n, [P, KC, VC], F16, "right") for n in ("wv_hi", "wv_lo"))
                with ExitStack() as stage:
                    w_hi, w_lo = (tensor(stage, n, [P, KC, QK], F16) for n in ("w_hi", "w_lo"))
                    project_qk(nc, x, wq, wkv, ident, c_hi, c_lo, w_hi, w_lo, wv_hi, wv_lo, qk_hi, qk_lo, sem)
                attend(nc, c_hi, c_lo, wv_hi, wv_lo, qk_hi, qk_lo, v_sb, ident, identb, causal, ones, c_hi, c_lo, sem)
            ffn = whole.enter_context(ExitStack())
            x2_hi, x2_lo = (tensor(ffn, n, [P, KC, T], F16, "right") for n in ("x2_hi", "x2_lo"))
            project_context(nc, c_hi, c_lo, wo, bo, x, x1_dram, ident, x2_hi, x2_lo, sem)
        wd_hi, wd_lo = (tensor(whole, n, [P, -(-inter // P), D], F16) for n in ("wd_hi", "wd_lo"))
        gate_and_up(nc, x2_hi, x2_lo, ((gate_q, gate_s, gate_z), (up_q, up_s, up_z), (down_q, down_s, down_z)),
                    ident, wd_hi, wd_lo, h_hi, h_lo, sem)
        ffn.close()
        project_down(nc, h_hi, h_lo, wd_hi, wd_lo, x1_dram, out, sem)


INPUTS = ["L0_attn_x", "L0_attn_Wq", "L0_attn_Wkv", "L0_attn_Wo", "L0_attn_bo", "L0_ffn_gate_Wq", "L0_ffn_up_Wq",
          "L0_ffn_down_Wq", "L0_ffn_gate_scale", "L0_ffn_gate_zero", "L0_ffn_up_scale", "L0_ffn_up_zero",
          "L0_ffn_down_scale", "L0_ffn_down_zero"]


def kernel(**inputs):
    import numpy as np
    from concourse import bacc
    from concourse.bass_utils import run_bass_kernel_spmd

    nc = bacc.Bacc("TRN2", target_bir_lowering=False, num_devices=1)
    arrays, args = {}, []
    shape = np.shape(inputs["L0_attn_x"])
    for name in INPUTS:
        a = np.ascontiguousarray(inputs[name])
        if name == "L0_attn_x":
            a = a.reshape(shape[1:])
        arrays[name] = a
        args.append(nc.dram_tensor(name, a.shape, mybir.dt.from_np(a.dtype), kind="ExternalInput").ap())
    args.append(nc.dram_tensor("out", shape[1:], F32, kind="ExternalOutput").ap())
    sandwich_layer(nc, *args)
    result = run_bass_kernel_spmd(nc, [arrays], core_ids=[0])
    return result.results[0]["out"].reshape(shape)
```
